# Optimizing a Trainium2 kernel written in Bass

```python
import numpy as np
import jax
import jax.numpy as jnp

def _softmax(x, axis=-1):
    return jax.nn.softmax(x, axis=axis)

def _gelu(x):
    return jax.nn.gelu(x, approximate=True)

def _silu(x):
    return jax.nn.silu(x)

def _sigmoid(x):
    return jax.nn.sigmoid(x)

def _layernorm(x, axis=-1, eps=1e-05):
    m = jnp.mean(x, axis=axis, keepdims=True)
    v = jnp.var(x, axis=axis, keepdims=True)
    return (x - m) / jnp.sqrt(v + eps)

def _scatter_add(tgt, idx, src, axis=0):
    return tgt.at[idx].add(src)

def _segment_sum(src, seg, n):
    return jax.ops.segment_sum(src, seg, n)
kernel_name = 'mk_adaln_ffn_d1_seqx_r4_cf9f3c'

def setup_inputs(seed: int=0):
    np.random.seed(seed)
    _w = jnp.asarray

    def _rec_inputs():
        import jax
        import jax.numpy as jnp
        _rk = jax.random.key(seed)
        x = -0.000125 + 0.9999 * jax.random.normal(jax.random.fold_in(_rk, 1), (128, 64, 256), jnp.float32)
        _lenS = 64 - jax.random.randint(jax.random.fold_in(_rk, 7), (128,), 0, max(1, 64 // 4) + 1, jnp.int32)
        _lenS2 = 64 - jax.random.randint(jax.random.fold_in(_rk, 8), (128,), 0, max(1, 64 // 4) + 1, jnp.int32)
        cond_1024 = 0.00513981 + 1.0024 * jax.random.normal(jax.random.fold_in(_rk, 11), (128, 256), jnp.float32)
        return (x, cond_1024)
    x, cond_1024 = _rec_inputs()

    def _L0_cond_setup():
        import jax, jax.numpy as jnp
        import numpy as np
        IN_FEATURES = 256
        OUT_FEATURES = 256
        BATCH = 32
        SEQ = 256
        EPS = 1e-08
        key = jax.random.key(seed)
        k1, k2, k3 = jax.random.split(key, 3)
        Efou = jax.random.normal(k1, (BATCH, SEQ, IN_FEATURES), dtype=jnp.float32)
        y = jax.random.normal(k2, (BATCH, IN_FEATURES), dtype=jnp.float32)
        weight = jax.random.normal(k3, (IN_FEATURES, OUT_FEATURES), dtype=jnp.float32)
        return {'Efou': Efou, 'y': y, 'weight': weight}
    _L0_cond_all = _L0_cond_setup()
    _L0_cond_in = {k: v for k, v in _L0_cond_all.items() if k in ('weight',)}
    del _L0_cond_all

    def _L0_ffn_setup():
        import jax, jax.numpy as jnp
        import numpy as np
        TOP_K = 2
        CAP_FACTOR = 1.25

        def _gelu(x):
            return 0.5 * x * (1.0 + jnp.tanh(jnp.sqrt(2.0 / jnp.pi) * (x + 0.044715 * x ** 3)))
        key = jax.random.key(seed)
        ks = jax.random.split(key, 6)
        B, S, D, F, E = (4, 512, 256, 1024, 8)
        return {'hidden_states': jax.random.normal(ks[0], (B, S, D), dtype=jnp.float32), 'wr': jax.random.normal(ks[1], (E, D), dtype=jnp.float32) * 0.02, 'w1': jax.random.normal(ks[2], (E, D, F), dtype=jnp.float32) * 0.02, 'b1': jnp.zeros((E, F), dtype=jnp.float32), 'w2': jax.random.normal(ks[3], (E, F, D), dtype=jnp.float32) * 0.02, 'b2': jnp.zeros((E, D), dtype=jnp.float32)}
    _L0_ffn_all = _L0_ffn_setup()
    _L0_ffn_in = {k: v for k, v in _L0_ffn_all.items() if k in ('wr', 'w1', 'b1', 'w2', 'b2')}
    del _L0_ffn_all
    return {'x': x, 'cond_1024': cond_1024, 'L0_cond_weight': _L0_cond_in['weight'], 'L0_ffn_wr': _L0_ffn_in['wr'], 'L0_ffn_w1': _L0_ffn_in['w1'], 'L0_ffn_b1': _L0_ffn_in['b1'], 'L0_ffn_w2': _L0_ffn_in['w2'], 'L0_ffn_b2': _L0_ffn_in['b2']}

def reference(x, cond_1024, L0_cond_weight, L0_ffn_wr, L0_ffn_w1, L0_ffn_b1, L0_ffn_w2, L0_ffn_b2):
    import jax
    import jax.numpy as jnp

    def _L0_cond_ref(Efou, y, weight):
        import jax, jax.numpy as jnp
        import numpy as np
        IN_FEATURES = 256
        OUT_FEATURES = 256
        BATCH = 32
        SEQ = 256
        EPS = 1e-08
        scale = 1.0 / np.sqrt(np.float32(weight.shape[0]))
        ys = y * scale
        d = jax.lax.rsqrt(jnp.einsum('bi,io->bo', ys * ys, weight * weight) + EPS)
        out = jnp.einsum('bsi,io->bso', Efou * ys[:, None, :], weight) * d[:, None, :]
        return out

    def _L0_ffn_ref(hidden_states, wr, w1, b1, w2, b2):
        import jax, jax.numpy as jnp
        import numpy as np
        TOP_K = 2
        CAP_FACTOR = 1.25

        def _gelu(x):
            return 0.5 * x * (1.0 + jnp.tanh(jnp.sqrt(2.0 / jnp.pi) * (x + 0.044715 * x ** 3)))
        B, S, D = hidden_states.shape
        E = wr.shape[0]
        x = hidden_states.reshape(-1, D)
        T = x.shape[0]
        logits = x @ wr.T
        vals, idx = jax.lax.top_k(logits, TOP_K)
        sparse = jnp.full((T, E), -jnp.inf, dtype=logits.dtype)
        sparse = sparse.at[jnp.arange(T)[:, None], idx].set(vals)
        gating = jax.nn.softmax(sparse, axis=-1)
        cap = max(8, int(max(1, T * TOP_K // E) * CAP_FACTOR))
        mask = (idx[:, :, None] == jnp.arange(E)).any(axis=1)
        pos = jnp.cumsum(mask.astype(jnp.int32), axis=0) - 1
        keep = mask & (pos < cap)
        slot = jnp.where(keep, pos, cap)
        e_grid = jnp.broadcast_to(jnp.arange(E)[None, :], (T, E))
        t_grid = jnp.broadcast_to(jnp.arange(T)[:, None], (T, E))
        dispatch = jnp.full((E, cap + 1), T, dtype=jnp.int32)
        dispatch = dispatch.at[e_grid, slot].set(t_grid)[:, :cap]
        x_pad = jnp.concatenate([x, jnp.zeros((1, D), x.dtype)], axis=0)
        g_pad = jnp.concatenate([gating, jnp.zeros((1, E), gating.dtype)], axis=0)
        xg = x_pad[dispatch]
        h = _gelu(jnp.einsum('ecd,edf->ecf', xg, w1) + b1[:, None, :])
        y = jnp.einsum('ecf,efd->ecd', h, w2) + b2[:, None, :]
        g = g_pad[dispatch, jnp.arange(E)[:, None]]
        wy = y * g[..., None]
        out = jax.ops.segment_sum(wy.reshape(-1, D), dispatch.reshape(-1), num_segments=T + 1)[:T]
        return out.reshape(B, S, D)
    x = x + _L0_ffn_ref(_L0_cond_ref(x, cond_1024, L0_cond_weight), L0_ffn_wr, L0_ffn_w1, L0_ffn_b1, L0_ffn_w2, L0_ffn_b2)
    return x

_drawn_inputs = setup_inputs


def setup_inputs(seed=0):
    import zlib

    import numpy as np

    out = dict(_drawn_inputs(seed))
    spreads = {'L0_ffn_b1': (0.0, 0.305), 'L0_ffn_b2': (0.0, 0.1)}
    factors = {}
    for name, (base, spread) in spreads.items():
        noise = np.random.default_rng([zlib.crc32(name.encode()), seed]).standard_normal(out[name].shape)
        drawn = base * np.exp(spread * noise) if base else spread * noise
        out[name] = jnp.asarray(drawn.astype(out[name].dtype))
    for name, factor in factors.items():
        out[name] = (out[name] * factor).astype(out[name].dtype)
    return out
```

```python
from contextlib import ExitStack

import numpy as np

import concourse.bass as bass
from concourse import mybir

F32 = mybir.dt.float32
F32R = mybir.dt.float32r
BF16 = mybir.dt.bfloat16
I32 = mybir.dt.int32
ALU = mybir.AluOpType
ACT = mybir.ActivationFunctionType
AX_X = mybir.AxisListType.X

P = 128
B, S, D = 128, 64, 256
E, F, TOP_K = 8, 1024, 2
T = B * S
CAP = max(8, int(max(1, T * TOP_K // E) * 1.25))
KC = D // P
FC = F // P
EPS = 1e-8

TILES = 4
ROWS = TILES * P
GROUPS = T // ROWS
GB = ROWS // S
BLOCKS = CAP // ROWS
AHEAD = 2
TABLE = (E * BLOCKS + AHEAD) * ROWS
assert CAP % ROWS == 0 and ROWS == 512

WCOLS = KC * F
PIECE = 512
PIECES = 2 * WCOLS // PIECE
NO_SLOT = float(1 << 20)
BIG = 3.0e38


def build(nc, x, cond, w, wr_t, w1, b1_t, w2, b2, ident, tri, expert_low, slot_base, token_ids,
          empty_table, out):
    hidden = nc.dram_tensor("hidden", [T + P, D], F32, kind="Internal").ap()
    table = nc.dram_tensor("table", [TABLE, 2], I32, kind="Internal").ap()

    x_rows = x.rearrange("b s d -> (b s) d").rearrange("(g j p) d -> g p j d", j=TILES, p=P)
    out_rows = out[0:T, :].rearrange("(g j p) d -> g p j d", j=TILES, p=P)
    hidden_rows = hidden[0:T, :].rearrange("(g j p) d -> g p j d", j=TILES, p=P)
    table_rows = table.rearrange("(b p j) c -> b p j c", p=P, j=TILES)
    w1_rows = w1.rearrange("e (k p) f -> e p k f", p=P)
    w2_rows = w2.rearrange("e (c p) d -> e p c d", p=P)

    with ExitStack() as ctx:
        def sb(name, shape, dt=F32):
            return ctx.enter_context(nc.sbuf_tensor("sb_" + name, shape, dt))

        def sem(name):
            return ctx.enter_context(nc.semaphore(name))

        bank = [ctx.enter_context(nc.psum_tensor(f"bank{i}", [P, 512], F32)) for i in range(8)]

        ident_sb = sb("ident", [P, P])
        tri_f = sb("tri_f", [P, P])
        tri_sb = sb("tri", [P, P], BF16)
        ones_sb = sb("ones", [P, P], BF16)
        low_sb = sb("expert_low", [P, E])
        base_sb = sb("slot_base", [P, E])
        ids_sb = sb("ids", [P, T // P], I32)
        cond_sb = sb("cond", [P, D])
        w_sb = sb("w", [P, KC, D])
        wsq_sb = sb("wsq", [P, KC, D])
        wr_sb = sb("wr", [P, KC, E])
        b1_sb = sb("b1", [P, E * FC])
        b2_sb = sb("b2", [P, E * D])
        b1_now = [sb(f"b1_now{u}", [P, FC]) for u in range(2)]
        zero_sb = sb("zero", [P, D])
        ys_t = sb("ys_t", [P, KC, B])
        ysq_t = sb("ysq_t", [P, KC, B])
        var_t = sb("var_t", [P, KC * B])
        root_t = sb("root_t", [P, KC * B])
        tmp_t = sb("tmp_t", [P, KC * B])
        d_t = sb("d_t", [P, KC, B])

        x_sb = [sb(f"x{u}", [P, TILES, D]) for u in range(2)]
        xs_t = sb("xs_t", [P, KC, ROWS])
        hid_t = sb("hid_t", [P, KC, ROWS])
        hid_sb = [sb(f"hid{u}", [P, TILES, D]) for u in range(2)]
        RE = [P, TILES, E]
        logits = sb("logits", RE)
        rest = sb("rest", RE)
        hit = sb("hit", RE)
        first = sb("first", RE)
        second = sb("second", RE)
        mask = sb("mask", RE, BF16)
        before = sb("before", [P, TILES + 1, E], BF16)
        slot_e = sb("slot_e", RE)
        over = sb("over", RE)
        top = sb("top", [P, 2, TILES])
        low = sb("low", [P, 2, TILES])
        gap = sb("gap", [P, TILES])
        ratio = sb("ratio", [P, TILES])
        total = sb("total", [P, TILES])
        slots = [sb(f"slots{u}", [P, 2, TILES], I32) for u in range(2)]
        pay = [sb(f"pay{u}", [P, 2, TILES, 2], I32) for u in range(2)]

        w_raw = sb("w_raw", [P, 2 * WCOLS])
        w_hi = [sb(f"w_hi{u}", [P, 2 * WCOLS], F32R) for u in range(2)]
        w_lo = [sb(f"w_lo{u}", [P, 2 * WCOLS], F32R) for u in range(2)]
        gather_ids = sb("gather_ids", [P, TILES, 2], I32)
        add_ids = sb("add_ids", [P, TILES, 2], I32)
        xg = sb("xg", [P, TILES, D])
        xt_hi = sb("xt_hi", [P, KC, ROWS], F32R)
        xt_lo = sb("xt_lo", [P, KC, ROWS], F32R)
        h_raw = [sb(f"h_raw{i}", [P, ROWS]) for i in range(2)]
        h_hi = [sb(f"h_hi{i}", [P, ROWS], F32R) for i in range(4)]
        h_lo = [sb(f"h_lo{i}", [P, ROWS], F32R) for i in range(4)]
        y_sb = [sb(f"y{s}", [P, D]) for s in range(TILES)]

        const_in = sem("const_in")
        table_empty = sem("table_empty")
        pad_zero = sem("pad_zero")
        set_dve = sem("set_dve")
        set_pe = sem("set_pe")
        set_act = sem("set_act")
        w_loaded = sem("w_loaded")
        x_loaded = [sem(f"x_loaded{u}") for u in range(2)]
        hid_stored = [sem(f"hid_stored{u}") for u in range(2)]
        scattered = [sem(f"scattered{u}") for u in range(2)]
        out_written = sem("out_written")
        added = sem("added")
        y_free = sem("y_free")
        t_done = sem("t_done")
        xs_ready = sem("xs_ready")
        m_done = sem("m_done")
        hid_ready = sem("hid_ready")
        l_done = sem("l_done")
        back_done = sem("back_done")
        hid_copied = sem("hid_copied")
        step = sem("step")
        mask_ready = sem("mask_ready")
        pos_done = sem("pos_done")
        gap_ready = sem("gap_ready")
        ratio_ready = sem("ratio_ready")
        pay_ready = sem("pay_ready")
        pool_paced = sem("pool_paced")
        bias_now = sem("bias_now")
        gather_listed = sem("gather_listed")
        add_listed = sem("add_listed")
        gathered = sem("gathered")
        w_hi_done = sem("w_hi_done")
        w_lo_done = sem("w_lo_done")
        xt_hi_done = sem("xt_hi_done")
        xt_ready = sem("xt_ready")
        s1_done = sem("s1_done")
        gelu_done = sem("gelu_done")
        hi_done = sem("hi_done")
        h_ready = sem("h_ready")
        s2_done = sem("s2_done")
        y_done = sem("y_done")
        y_biased = sem("y_biased")
        y_ready = sem("y_ready")

        CONSTS = 10
        out_filled = 16 * (1 + GROUPS)

        def groups(eng, body):
            for g in range(2):
                body(g, g, 0)
            with eng.Fori(1, GROUPS // 2 - 1) as t:
                for u in range(2):
                    body(t * 2 + u, u, t)
            for g in range(GROUPS - 2, GROUPS):
                body(g, g % 2, g // 2)

        def chunk(tile, k):
            return tile[:, k, :]

        block = ctx.enter_context(nc.Block())

        @block.sync
        def _(sp):
            sp.dma_start(cond_sb[:, :], cond).then_inc(const_in, 16)
            sp.dma_start(ident_sb[:, :], ident).then_inc(const_in, 16)
            sp.dma_start(w_sb[:, :, :], w.rearrange("(k p) o -> p k o", p=P)).then_inc(const_in, 16)
            for g in range(2):
                sp.dma_start(x_sb[g][:, :, :], x_rows[g, :, :, :]).then_inc(x_loaded[g], 16)
            sp.dma_start(table, empty_table).then_inc(table_empty, 16)
            sp.dma_start(wr_sb[:, :, :], wr_t.rearrange("(k p) e -> p k e", p=P)).then_inc(const_in, 16)
            sp.dma_start(tri_f[:, :], tri).then_inc(const_in, 16)
            sp.dma_start(low_sb[:, :], expert_low).then_inc(const_in, 16)
            sp.dma_start(base_sb[:, :], slot_base).then_inc(const_in, 16)
            sp.dma_start(ids_sb[:, :], token_ids).then_inc(const_in, 16)
            sp.dma_start(b1_sb[:, :], b1_t).then_inc(const_in, 16)
            sp.dma_start(b2_sb[:, :], b2.rearrange("e d -> (e d)").partition_broadcast(P)).then_inc(const_in, 16)
            sp.wait_ge(set_dve, 1)
            sp.dma_start(hidden[T:T + P, :], zero_sb[:, :]).then_inc(pad_zero, 16)
            sp.dma_start(out[T:T + P, :], zero_sb[:, :]).then_inc(out_written, 16)

            def load_weights(e):
                sp.dma_start(w_raw[:, 0:WCOLS].rearrange("p (k f) -> p k f", k=KC),
                             w1_rows[e, :, :, :]).then_inc(w_loaded, 16)
                sp.dma_start(w_raw[:, WCOLS:2 * WCOLS].rearrange("p (c d) -> p c d", c=FC),
                             w2_rows[e, :, :, :]).then_inc(w_loaded, 16)

            load_weights(0)

            def stage1(g, u, t, refill=True):
                sp.wait_ge(x_loaded[u], 16 * (t + 1))
                sp.dma_start(out_rows[g, :, :, :], x_sb[u][:, :, :]).then_inc(out_written, 16)
                sp.wait_ge(hid_copied, 2 * (g + 1))
                sp.dma_start(hidden_rows[g, :, :, :], hid_sb[u][:, :, :]).then_inc(hid_stored[u], 16)
                if refill:
                    sp.wait_ge(out_written, 16 * (g + 2))
                    sp.dma_start(x_sb[u][:, :, :], x_rows[g + 2, :, :, :]).then_inc(x_loaded[u], 16)

            for g in range(2):
                stage1(g, g, 0)
            with sp.Fori(1, GROUPS // 2 - 1) as t:
                for u in range(2):
                    stage1(t * 2 + u, u, t)
            for g in range(GROUPS - 2, GROUPS):
                stage1(g, g % 2, g // 2, refill=False)

            for u in range(2):
                sp.wait_ge(scattered[u], 16 * 2 * TILES * (GROUPS // 2))
            sp.dma_start(gather_ids[:, :, :], table_rows[0, :, :, :]).then_inc(gather_listed, 16)
            sp.wait_ge(gathered, 16 * TILES)
            sp.dma_start(gather_ids[:, :, :], table_rows[1, :, :, :]).then_inc(gather_listed, 16)
            with sp.Fori(0, E) as e:
                sp.wait_ge(w_lo_done, PIECES * (e + 1))
                load_weights((e + 1) % E)
                with sp.Fori(0, BLOCKS) as j:
                    b = e * BLOCKS + j
                    sp.wait_ge(gathered, 16 * TILES * (b + 2))
                    sp.dma_start(gather_ids[:, :, :], table_rows[b + 2, :, :, :]).then_inc(gather_listed, 16)
                    sp.wait_ge(y_free, TILES * (b + 1))
                    sp.dma_start(add_ids[:, :, :], table_rows[b, :, :, :]).then_inc(add_listed, 16)
            sp.wait_ge(added, 16 * TILES * E * BLOCKS)
            sp.wait_ge(w_loaded, 32 * (E + 1))
            sp.wait_ge(gathered, 16 * TILES * (E * BLOCKS + AHEAD))

        @block.gpsimd
        def _(pool):
            pool.wait_ge(table_empty, 16)

            def scatter(g, u, t):
                pool.wait_ge(pay_ready, g + 1)
                pool.sem_inc(pool_paced)
                for j in range(TILES):
                    for c in range(TOP_K):
                        pool.indirect_dma_start(
                            table, bass.IndirectOffsetOnAxis(slots[u][:, c, j:j + 1], axis=0),
                            pay[u][:, c, j, :], None, bounds_check=TABLE - 1, oob_is_err=False,
                        ).then_inc(scattered[u], 16)

            groups(pool, scatter)

            def gather():
                for s in range(TILES):
                    pool.indirect_dma_start(
                        xg[:, s, :], None, hidden,
                        bass.IndirectOffsetOnAxis(gather_ids[:, s, 0:1], axis=0),
                    ).then_inc(gathered, 16)

            pool.wait_ge(pad_zero, 16)
            for u in range(2):
                pool.wait_ge(hid_stored[u], 16 * (GROUPS // 2))
            pool.sem_inc(y_free, TILES)
            for b in range(AHEAD):
                pool.wait_ge(gather_listed, 16 * (b + 1))
                pool.wait_ge(t_done, GROUPS + b)
                gather()
            pool.wait_ge(out_written, out_filled)
            with pool.Fori(0, E * BLOCKS) as b:
                pool.wait_ge(gather_listed, 16 * (b + 3))
                pool.wait_ge(t_done, b + (GROUPS + 2))
                pool.sem_inc(pool_paced)
                gather()
                pool.wait_ge(add_listed, 16 * (b + 1))
                for s in range(TILES):
                    pool.wait_ge(y_ready, b * TILES + (s + 1))
                    pool.sem_inc(pool_paced)
                    pool.indirect_dma_start(
                        out, bass.IndirectOffsetOnAxis(add_ids[:, s, 0:1], axis=0),
                        y_sb[s][:, :], None, compute_op=ALU.add,
                    ).then_inc(added, 16)
                    pool.wait_ge(added, 16 * (b * TILES) + 16 * (s + 1))
                    pool.sem_inc(y_free)

        @block.tensor
        def _(pe):
            pe.wait_ge(const_in, 16 * CONSTS)
            for k in range(KC):
                last = pe.transpose(bank[7][:, k * P:(k + 1) * P], cond_sb[:, k * P:(k + 1) * P], ident_sb[:, :])
            last.then_inc(set_pe, 1)
            pe.wait_ge(set_dve, 6)
            for o in range(KC):
                for k in range(KC):
                    last = pe.matmul(bank[6][:, o * B:(o + 1) * B], wsq_sb[:, k, o * P:(o + 1) * P],
                                     ysq_t[:, k, :], start=(k == 0), stop=(k == KC - 1))
            last.then_inc(set_pe, 1)

            def transpose_x(u, count):
                pe.wait_ge(x_loaded[u], count)
                for k in range(KC):
                    for j in range(TILES):
                        mm = pe.transpose(bank[k][:, j * P:(j + 1) * P], x_sb[u][:, j, k * P:(k + 1) * P],
                                          ident_sb[:, :])
                mm.then_inc(t_done, 1)

            transpose_x(0, 16)

            def stage1(g, u, t, more=True):
                pe.wait_ge(xs_ready, KC * (g + 1))
                for o in range(KC):
                    for k in range(KC):
                        mm = pe.matmul(bank[2 + o][:, :], w_sb[:, k, o * P:(o + 1) * P], xs_t[:, k, :],
                                       start=(k == 0), stop=(k == KC - 1))
                    mm.then_inc(m_done, 1)
                if more:
                    transpose_x(1 - u, 16 * (t + u + 1))
                pe.wait_ge(hid_ready, KC * (g + 1))
                for j in range(TILES):
                    for k in range(KC):
                        mm = pe.matmul(bank[6][:, j * E:(j + 1) * E], hid_t[:, k, j * P:(j + 1) * P],
                                       wr_sb[:, k, :], start=(k == 0), stop=(k == KC - 1))
                mm.then_inc(l_done, 1)
                if not (isinstance(g, int) and g == 0):
                    pe.wait_ge(hid_copied, 2 * g)
                for j in range(TILES):
                    for k in range(KC):
                        mm = pe.transpose(bank[4 + j // 2][:, (j % 2) * D + k * P:(j % 2) * D + (k + 1) * P],
                                          hid_t[:, k, j * P:(j + 1) * P], ident_sb[:, :])
                mm.then_inc(back_done, 1)
                pe.wait_ge(mask_ready, g + 1)
                pe.matmul(bank[7][:, 0:TILES * E], tri_sb[:, :], mask[:, :, :].rearrange("p j e -> p (j e)"),
                          start=True, stop=False)
                pe.matmul(bank[7][:, 0:TILES * E], ones_sb[:, :],
                          before[:, 0:TILES, :].rearrange("p j e -> p (j e)"),
                          start=False, stop=True).then_inc(pos_done, 1)

            for g in range(2):
                stage1(g, g, 0)
            with pe.Fori(1, GROUPS // 2 - 1) as t:
                for u in range(2):
                    stage1(t * 2 + u, u, t)
            for g in range(GROUPS - 2, GROUPS):
                stage1(g, g % 2, g // 2, more=(g < GROUPS - 1))

            def transpose_block(b):
                pe.wait_ge(gathered, 16 * TILES * (b + 1))
                for k in range(KC):
                    for s in range(TILES):
                        mm = pe.transpose(bank[k][:, s * P:(s + 1) * P], xg[:, s, k * P:(k + 1) * P],
                                          ident_sb[:, :])
                mm.then_inc(t_done, 1)

            def second(u, f, first_of_y):
                for s in range(TILES):
                    hi = h_hi[f % 4][:, s * P:(s + 1) * P]
                    lo = h_lo[f % 4][:, s * P:(s + 1) * P]
                    cols = slice(WCOLS + f * D, WCOLS + (f + 1) * D)
                    y = bank[4 + s][:, 0:D]
                    pe.matmul(y, hi, w_hi[u][:, cols], start=(f == 0), stop=False)
                    pe.matmul(y, hi, w_lo[u][:, cols], start=False, stop=False)
                    mm = pe.matmul(y, lo, w_hi[u][:, cols], start=False, stop=(f == FC - 1))
                    if f == FC - 1:
                        mm.then_inc(y_done, 1)
                if f < FC - 1:
                    mm.then_inc(s2_done, 1)

            transpose_block(0)
            with pe.Fori(0, E // 2) as pair:
                for u in range(2):
                    with pe.Fori(0, BLOCKS) as j:
                        b = pair * (2 * BLOCKS) + j + u * BLOCKS
                        pe.wait_ge(w_lo_done, PIECES * (pair * 2 + u + 1))
                        pe.wait_ge(xt_ready, KC * (b + 1))
                        for f in range(FC + 2):
                            if f < FC:
                                if f >= 2:
                                    pe.wait_ge(gelu_done, b * FC + (f - 1))
                                h = bank[2 + f % 2][:, :]
                                for k in range(KC):
                                    cols = slice(k * F + f * P, k * F + (f + 1) * P)
                                    pe.matmul(h, w_hi[u][:, cols], xt_hi[:, k, :], start=(k == 0), stop=False)
                                    pe.matmul(h, w_hi[u][:, cols], xt_lo[:, k, :], start=False, stop=False)
                                    mm = pe.matmul(h, w_lo[u][:, cols], xt_hi[:, k, :], start=False,
                                                   stop=(k == KC - 1))
                                mm.then_inc(s1_done, 1)
                            if f == 4:
                                transpose_block(b + 1)
                            if f >= 2:
                                pe.wait_ge(h_ready, b * FC + (f - 1))
                                second(u, f - 2, f == 2)

        @block.scalar
        def _(act):
            act.wait_ge(set_dve, 7)
            act.activation(root_t[:, :], var_t[:, :], ACT.Sqrt).then_inc(set_act, 1)

            def split_piece(u, i, n_loaded):
                if i == 0:
                    act.wait_ge(w_loaded, n_loaded)
                cols = slice(i * PIECE, (i + 1) * PIECE)
                act.copy(w_hi[u][:, cols], w_raw[:, cols]).then_inc(w_hi_done, 1)

            for i in range(PIECES):
                split_piece(0, i, 32)

            def stage1(g, u, t):
                act.wait_ge(back_done, g + 1)
                if not (isinstance(t, int) and t == 0):
                    act.wait_ge(hid_stored[u], 16 * t)
                for h in range(2):
                    act.copy(hid_sb[u][:, 2 * h:2 * h + 2, :].rearrange("p j d -> p (j d)"),
                             bank[4 + h][:, :]).then_inc(hid_copied, 1)
                act.wait_ge(gap_ready, g + 1)
                act.activation(ratio[:, :], gap[:, :], ACT.Exp).then_inc(ratio_ready, 1)

            groups(act, stage1)

            def split_rows(b):
                act.wait_ge(t_done, b + (GROUPS + 1))
                for k in range(KC):
                    act.copy(xt_hi[:, k, :], bank[k][:, :]).then_inc(xt_hi_done, 1)

            split_rows(0)
            with act.Fori(0, E // 2) as pair:
                for u in range(2):
                    act.copy(b1_now[u][:, :], b1_sb[:, bass.ds((pair * 2 + u) * FC, FC)]).then_inc(bias_now, 1)
                    act.wait_ge(bias_now, pair * 2 + (u + 1))
                    for j in range(BLOCKS):
                        e = pair * 2 + u
                        b = e * BLOCKS + j
                        for f in range(FC):
                            act.wait_ge(s1_done, b * FC + (f + 1))
                            if f >= 2:
                                act.wait_ge(h_ready, b * FC + (f - 1))
                            act.activation(h_raw[f % 2][:, :], bank[2 + f % 2][:, :], ACT.Gelu_apprx_tanh,
                                           bias=b1_now[u][:, f:f + 1]).then_inc(gelu_done, 1)
                            if j * 2 < PIECES and f in (2, 4):
                                split_piece(1 - u, j * 2 + (f == 4), 32 * (e + 2))
                        split_rows(b + 1)

        @block.vector
        def _(dve):
            dve.memset(zero_sb[:, :], 0.0).then_inc(set_dve, 1)
            dve.memset(ones_sb[:, :], 1.0)
            dve.memset(before[:, :, :], 0.0)
            dve.wait_ge(const_in, 16 * CONSTS)
            dve.tensor_copy(tri_sb[:, :], tri_f[:, :])
            scale = 1.0 / float(np.sqrt(np.float32(D)))
            dve.tensor_tensor(wsq_sb[:, :, :], w_sb[:, :, :], w_sb[:, :, :], ALU.mult).then_inc(set_dve, 1)
            dve.wait_ge(set_pe, 1)
            ys_flat = ys_t[:, :, :].rearrange("p k b -> p (k b)")
            ysq_flat = ysq_t[:, :, :].rearrange("p k b -> p (k b)")
            d_flat = d_t[:, :, :].rearrange("p k b -> p (k b)")
            dve.tensor_scalar(ys_flat, bank[7][:, 0:KC * B], scale, None, ALU.mult).then_inc(set_dve, 1)
            dve.wait_ge(set_dve, 3)
            dve.tensor_tensor(ysq_flat, ys_flat, ys_flat, ALU.mult).then_inc(set_dve, 3)
            dve.wait_ge(set_pe, 2)
            dve.tensor_scalar(var_t[:, :], bank[6][:, 0:KC * B], EPS, None, ALU.add).then_inc(set_dve, 1)
            dve.wait_ge(set_act, 1)
            dve.reciprocal(root_t[:, :], root_t[:, :]).then_inc(set_dve, 1)
            dve.wait_ge(set_dve, 8)
            dve.tensor_tensor(tmp_t[:, :], root_t[:, :], root_t[:, :], ALU.mult).then_inc(set_dve, 1)
            dve.wait_ge(set_dve, 9)
            dve.tensor_tensor(tmp_t[:, :], tmp_t[:, :], var_t[:, :], ALU.mult).then_inc(set_dve, 1)
            dve.wait_ge(set_dve, 10)
            dve.tensor_scalar(tmp_t[:, :], tmp_t[:, :], -0.5, 1.5, ALU.mult, ALU.add).then_inc(set_dve, 1)
            dve.wait_ge(set_dve, 11)
            dve.tensor_tensor(d_flat, tmp_t[:, :], root_t[:, :], ALU.mult).then_inc(set_dve, 1)
            dve.wait_ge(set_dve, 12)

            def split_piece(u, i, count):
                cols = slice(i * PIECE, (i + 1) * PIECE)
                dve.wait_ge(w_hi_done, count)
                dve.tensor_tensor(w_lo[u][:, cols], w_raw[:, cols], w_hi[u][:, cols].bitcast(F32),
                                  ALU.subtract).then_inc(w_lo_done, 1)

            def by_batch(tile, k, g):
                return tile[:, k, bass.ds(g * GB, GB)].unsqueeze(2).to_broadcast([P, GB, S])

            def scale_x(g):
                dve.wait_ge(t_done, g + 1)
                for k in range(KC):
                    dve.tensor_tensor(xs_t[:, k, :].rearrange("p (b s) -> p b s", s=S),
                                      bank[k][:, :].rearrange("p (b s) -> p b s", s=S),
                                      by_batch(ys_t, k, g), ALU.mult).then_inc(xs_ready, 1)

            scale_x(0)
            for i in range(PIECES):
                split_piece(0, i, i + 1)

            STEPS = 21

            def stage1(g, u, t, more=True):
                n = [0]

                def then(ins):
                    n[0] += 1
                    ins.then_inc(step, 1)
                    dve.wait_ge(step, g * STEPS + n[0])

                def over_e(a):
                    return a.unsqueeze(2).to_broadcast(RE)

                low3 = low_sb[:, :].unsqueeze(1).to_broadcast(RE)
                base3 = base_sb[:, :].unsqueeze(1).to_broadcast(RE)

                for o in range(KC):
                    dve.wait_ge(m_done, KC * g + (o + 1))
                    dve.tensor_tensor(hid_t[:, o, :].rearrange("p (b s) -> p b s", s=S),
                                      bank[2 + o][:, :].rearrange("p (b s) -> p b s", s=S),
                                      by_batch(d_t, o, g), ALU.mult).then_inc(hid_ready, 1)
                if more:
                    scale_x(g + 1)

                dve.wait_ge(l_done, g + 1)
                then(dve.tensor_copy(logits[:, :, :].rearrange("p j e -> p (j e)"), bank[6][:, 0:TILES * E]))

                def choose(c, values, one_hot):
                    then(dve.tensor_reduce(top[:, c, :], values, AX_X, ALU.max))
                    then(dve.tensor_tensor(hit[:, :, :], values, over_e(top[:, c, :]), ALU.is_equal))
                    then(dve.tensor_tensor(hit[:, :, :], hit[:, :, :], low3, ALU.mult))
                    then(dve.tensor_reduce(low[:, c, :], hit[:, :, :], AX_X, ALU.min))
                    then(dve.tensor_tensor(one_hot, low3, over_e(low[:, c, :]), ALU.is_equal))

                choose(0, logits[:, :, :], first[:, :, :])
                then(dve.scalar_tensor_tensor(rest[:, :, :], first[:, :, :], -BIG, logits[:, :, :],
                                              ALU.mult, ALU.add))
                choose(1, rest[:, :, :], second[:, :, :])
                if not (isinstance(g, int) and g == 0):
                    dve.wait_ge(ratio_ready, g)
                dve.tensor_tensor(gap[:, :], top[:, 1, :], top[:, 0, :], ALU.subtract).then_inc(gap_ready, 1)
                then(dve.tensor_tensor(mask[:, :, :], first[:, :, :], second[:, :, :], ALU.add))
                for j in range(TILES):
                    ins = dve.tensor_tensor(before[:, j + 1, :], before[:, j, :], mask[:, j, :], ALU.add)
                    if j < TILES - 1:
                        then(ins)
                ins.then_inc(mask_ready, 1)

                dve.wait_ge(ratio_ready, g + 1)
                then(dve.tensor_scalar(total[:, :], ratio[:, :], 1.0, None, ALU.add))
                then(dve.reciprocal(total[:, :], total[:, :]))
                if not (isinstance(t, int) and t == 0):
                    dve.wait_ge(scattered[u], (16 * TOP_K * TILES) * t)
                gates = pay[u].bitcast(F32)
                dve.tensor_copy(gates[:, 0, :, 1], total[:, :])
                dve.tensor_tensor(gates[:, 1, :, 1], total[:, :], ratio[:, :], ALU.mult)
                for c in range(TOP_K):
                    dve.tensor_copy(pay[u][:, c, :, 0], ids_sb[:, bass.ds(g * TILES, TILES)])

                dve.wait_ge(pos_done, g + 1)
                pos = bank[7][:, 0:TILES * E].rearrange("p (j e) -> p j e", e=E)
                dve.tensor_scalar(over[:, :, :], pos, float(CAP), NO_SLOT, ALU.is_gt, ALU.mult)
                then(dve.tensor_tensor(slot_e[:, :, :], pos, base3, ALU.add))
                dve.tensor_copy(before[:, 0, :], before[:, TILES, :])
                then(dve.tensor_tensor(slot_e[:, :, :], slot_e[:, :, :], over[:, :, :], ALU.add))
                dve.tensor_tensor(hit[:, :, :], first[:, :, :], slot_e[:, :, :], ALU.mult)
                then(dve.tensor_tensor(rest[:, :, :], second[:, :, :], slot_e[:, :, :], ALU.mult))
                with nc.allow_low_precision(reason="whole numbers below 2**24"):
                    dve.tensor_reduce(slots[u][:, 0, :], hit[:, :, :], AX_X, ALU.add)
                    dve.tensor_reduce(slots[u][:, 1, :], rest[:, :, :], AX_X, ALU.add).then_inc(pay_ready, 1)
                assert n[0] == STEPS, n[0]

            for g in range(2):
                stage1(g, g, 0)
            with dve.Fori(1, GROUPS // 2 - 1) as t:
                for u in range(2):
                    stage1(t * 2 + u, u, t)
            for g in range(GROUPS - 2, GROUPS):
                stage1(g, g % 2, g // 2, more=(g < GROUPS - 1))

            def split_rows(b):
                for k in range(KC):
                    dve.wait_ge(xt_hi_done, b * KC + (k + 1))
                    dve.tensor_tensor(xt_lo[:, k, :], bank[k][:, :], xt_hi[:, k, :].bitcast(F32),
                                      ALU.subtract).then_inc(xt_ready, 1)

            split_rows(0)
            with dve.Fori(0, E // 2) as pair:
                for u in range(2):
                    for j in range(BLOCKS):
                        e = pair * 2 + u
                        b = e * BLOCKS + j
                        for f in range(FC):
                            dve.wait_ge(gelu_done, b * FC + (f + 1))
                            if f >= 4:
                                dve.wait_ge(s2_done, b * (FC - 1) + (f - 3))
                            dve.tensor_copy(h_hi[f % 4][:, :], h_raw[f % 2][:, :]).then_inc(hi_done, 1)
                            dve.wait_ge(hi_done, b * FC + (f + 1))
                            dve.tensor_tensor(h_lo[f % 4][:, :], h_raw[f % 2][:, :],
                                              h_hi[f % 4][:, :].bitcast(F32), ALU.subtract).then_inc(h_ready, 1)
                            if j * 2 < PIECES and f in (3, 5):
                                i = j * 2 + (f == 5)
                                split_piece(1 - u, i, PIECES * (e + 1) + (i + 1))
                        split_rows(b + 1)
                        for s in range(TILES):
                            dve.wait_ge(y_done, b * TILES + (s + 1))
                            dve.wait_ge(y_free, b * TILES + (s + 1))
                            dve.tensor_tensor(y_sb[s][:, :], bank[4 + s][:, 0:D], b2_sb[:, bass.ds(e * D, D)],
                                              ALU.add).then_inc(y_biased, 1)
                        dve.wait_ge(add_listed, 16 * (b + 1))
                        for s in range(TILES):
                            dve.wait_ge(y_biased, b * TILES + (s + 1))
                            dve.tensor_scalar(y_sb[s][:, :], y_sb[s][:, :], add_ids.bitcast(F32)[:, s, 1:2],
                                              None, ALU.mult).then_inc(y_ready, 1)


def constants():
    p = np.arange(P)
    empty = np.zeros((TABLE, 2), np.int32)
    empty[:, 0] = T + (np.arange(TABLE) % ROWS) // TILES
    return {
        "ident": np.eye(P, dtype=np.float32),
        "tri": (p[:, None] <= p[None, :]).astype(np.float32),
        "expert_low": np.tile(np.arange(E, dtype=np.float32) - E, (P, 1)),
        "slot_base": np.tile(np.arange(E, dtype=np.float32) * CAP - 1, (P, 1)),
        "token_ids": (np.arange(T // P, dtype=np.int32)[None, :] * P + p[:, None].astype(np.int32)),
        "empty_table": empty,
    }


def kernel(x, cond_1024, L0_cond_weight, L0_ffn_wr, L0_ffn_w1, L0_ffn_b1, L0_ffn_w2, L0_ffn_b2):
    import concourse.bacc as bacc
    from concourse.bass_utils import run_bass_kernel_spmd

    arrays = {
        "x": x,
        "cond": cond_1024,
        "w": L0_cond_weight,
        "wr_t": np.asarray(L0_ffn_wr).T,
        "w1": L0_ffn_w1,
        "b1_t": np.asarray(L0_ffn_b1).reshape(E, FC, P).transpose(2, 0, 1).reshape(P, E * FC),
        "w2": L0_ffn_w2,
        "b2": L0_ffn_b2,
        **constants(),
    }
    arrays = {f"in_{k}": np.ascontiguousarray(v) for k, v in arrays.items()}
    nc = bacc.Bacc("TRN2", target_bir_lowering=False, num_devices=1)
    args = [nc.dram_tensor(k, v.shape, mybir.dt.from_np(v.dtype), kind="ExternalInput").ap()
            for k, v in arrays.items()]
    out = nc.dram_tensor("out_rows", (T + P, D), F32, kind="ExternalOutput").ap()
    build(nc, *args, out)
    r = run_bass_kernel_spmd(nc, [arrays], core_ids=[0])
    return r.results[0]["out_rows"][:T].reshape(B, S, D)
```

```python
from contextlib import ExitStack

import numpy as np

import concourse.bass as bass
from concourse import mybir

F32 = mybir.dt.float32
F32R = mybir.dt.float32r
BF16 = mybir.dt.bfloat16
I32 = mybir.dt.int32
ALU = mybir.AluOpType
ACT = mybir.ActivationFunctionType
AX_X = mybir.AxisListType.X

P = 128
B, S, D = 128, 64, 256
E, F, TOP_K = 8, 1024, 2
T = B * S
CAP = max(8, int(max(1, T * TOP_K // E) * 1.25))
KC = D // P
FC = F // P
EPS = 1e-8

TILES = 4
ROWS = TILES * P
GROUPS = T // ROWS
GB = ROWS // S
SUBS = 2
SLOTS = SUBS * P
BLOCKS = CAP // SLOTS
LEAST = 3
AHEAD = 2
TABLE = (E * BLOCKS + AHEAD) * SLOTS
LAG = 3
RING = 4
assert CAP % SLOTS == 0 and ROWS == 512 and T % (4 * ROWS) == 0

WCOLS = KC * F
PIECE = 512
PIECES = 2 * WCOLS // PIECE
NO_SLOT = float(1 << 20)
BIG = 3.0e38


def build(nc, x, cond, w, wr_t, w1, b1_t, w2, b2, ident, tri, expert_low, slot_base, token_ids,
          plan_consts, empty_table, out):
    hidden = nc.dram_tensor("hidden", [T + P, D], F32, kind="Internal").ap()
    table = nc.dram_tensor("table", [TABLE, 2], I32, kind="Internal").ap()

    x_rows = x.rearrange("b s d -> (b s) d").rearrange("(g j p) d -> g p j d", j=TILES, p=P)
    out_rows = out[0:T, :].rearrange("(g j p) d -> g p j d", j=TILES, p=P)
    hidden_rows = hidden[0:T, :].rearrange("(g j p) d -> g p j d", j=TILES, p=P)
    table_rows = table.rearrange("(b p j) c -> b p j c", p=P, j=SUBS)
    w1_rows = w1.rearrange("e (k p) f -> e p k f", p=P)
    w2_rows = w2.rearrange("e (c p) d -> e p c d", p=P)

    with ExitStack() as ctx:
        def sb(name, shape, dt=F32):
            return ctx.enter_context(nc.sbuf_tensor("sb_" + name, shape, dt))

        def sem(name):
            return ctx.enter_context(nc.semaphore(name))

        bank = [ctx.enter_context(nc.psum_tensor(f"bank{i}", [P, 512], F32)) for i in range(8)]

        ident_sb = sb("ident", [P, P])
        tri_f = sb("tri_f", [P, P])
        tri_sb = sb("tri", [P, P], BF16)
        ones_sb = sb("ones", [P, P], BF16)
        low_sb = sb("expert_low", [P, E])
        base_sb = sb("slot_base", [P, E])
        ids_sb = sb("ids", [P, T // P], I32)
        cond_sb = sb("cond", [P, D])
        w_sb = sb("w", [P, KC, D])
        wsq_sb = sb("wsq", [P, KC, D])
        wr_sb = sb("wr", [P, KC, E])
        b1_sb = sb("b1", [P, E * FC])
        b2_sb = sb("b2", [P, E * D])
        warm_sb = sb("warm", [P, 1])
        b1_now = [sb(f"b1_now{u}", [P, FC]) for u in range(2)]
        zero_sb = sb("zero", [P, D])
        plan_sb = sb("plan_consts", [P, BLOCKS + (E + 1) * E])
        steps_e = sb("steps_e", [P, E, BLOCKS])
        count_e = sb("count_e", [P, E])
        sums_e = sb("sums_e", [P, E + 1, E])
        plan = sb("plan", [P, E + E + 1], I32)
        ys_t = sb("ys_t", [P, KC, B])
        ysq_t = sb("ysq_t", [P, KC, B])
        var_t = sb("var_t", [P, KC * B])
        root_t = sb("root_t", [P, KC * B])
        tmp_t = sb("tmp_t", [P, KC * B])
        d_t = sb("d_t", [P, KC, B])

        x_sb = [sb(f"x{u}", [P, TILES, D]) for u in range(2)]
        xs_t = sb("xs_t", [P, KC, ROWS])
        hid_t = sb("hid_t", [P, KC, ROWS])
        hid_sb = [sb(f"hid{u}", [P, TILES, D]) for u in range(2)]
        RE = [P, TILES, E]
        logits = sb("logits", RE)
        rest = sb("rest", RE)
        hit = sb("hit", RE)
        first = sb("first", RE)
        second = sb("second", RE)
        mask = sb("mask", RE, BF16)
        before = sb("before", [P, TILES + 1, E], BF16)
        slot_e = sb("slot_e", RE)
        over = sb("over", RE)
        top = sb("top", [P, 2, TILES])
        low = sb("low", [P, 2, TILES])
        gap = sb("gap", [P, TILES])
        ratio = sb("ratio", [P, TILES])
        total = sb("total", [P, TILES])
        slots = [sb(f"slots{u}", [P, 2, TILES], I32) for u in range(2)]
        pay = [sb(f"pay{u}", [P, 2, TILES, 2], I32) for u in range(2)]

        w_raw = sb("w_raw", [P, 2 * WCOLS])
        w_hi = [sb(f"w_hi{u}", [P, 2 * WCOLS], F32R) for u in range(2)]
        w_lo = [sb(f"w_lo{u}", [P, 2 * WCOLS], F32R) for u in range(2)]
        gather_ids = sb("gather_ids", [P, SUBS, 2], I32)
        add_ids = sb("add_ids", [P, SUBS, 2], I32)
        xg = sb("xg", [P, SUBS, D])
        XT = KC * SLOTS
        xt_hi = sb("xt_hi", [P, 2 * XT], F32R)
        xt_lo = sb("xt_lo", [P, 2 * XT], F32R)
        h_raw = [sb(f"h_raw{i}", [P, SLOTS]) for i in range(RING)]
        h_hi = [sb(f"h_hi{i}", [P, SLOTS], F32R) for i in range(RING)]
        h_lo = [sb(f"h_lo{i}", [P, SLOTS], F32R) for i in range(RING)]
        y_sb = [sb(f"y{s}", [P, D]) for s in range(SUBS)]

        const_in = sem("const_in")
        table_empty = sem("table_empty")
        pad_zero = sem("pad_zero")
        set_dve = sem("set_dve")
        set_pe = sem("set_pe")
        set_act = sem("set_act")
        w_loaded = sem("w_loaded")
        x_loaded = [sem(f"x_loaded{u}") for u in range(2)]
        hid_stored = [sem(f"hid_stored{u}") for u in range(2)]
        scattered = [sem(f"scattered{u}") for u in range(2)]
        out_written = sem("out_written")
        added = sem("added")
        y_free = sem("y_free")
        t_done = sem("t_done")
        xs_ready = sem("xs_ready")
        m_done = sem("m_done")
        hid_ready = sem("hid_ready")
        l_done = sem("l_done")
        back_done = sem("back_done")
        hid_copied = sem("hid_copied")
        step = sem("step")
        chain = sem("chain")
        mask_ready = sem("mask_ready")
        pos_done = sem("pos_done")
        gap_ready = sem("gap_ready")
        ratio_ready = sem("ratio_ready")
        pay_ready = sem("pay_ready")
        pool_paced = sem("pool_paced")
        sp_paced = sem("sp_paced")
        bias_now = sem("bias_now")
        totals_done = sem("totals_done")
        plan_step = sem("plan_step")
        plan_ready = sem("plan_ready")
        gather_listed = sem("gather_listed")
        add_listed = sem("add_listed")
        gathered = sem("gathered")
        w_hi_done = sem("w_hi_done")
        w_lo_done = sem("w_lo_done")
        xt_hi_done = sem("xt_hi_done")
        xt_ready = sem("xt_ready")
        s1_done = sem("s1_done")
        gelu_done = sem("gelu_done")
        hi_done = sem("hi_done")
        h_ready = sem("h_ready")
        s2_done = sem("s2_done")
        y_done = sem("y_done")
        y_biased = sem("y_biased")
        y_ready = sem("y_ready")

        CONSTS = 11
        SPLIT_AT = (1, 3, 5, 7)
        assert PIECES == 2 * len(SPLIT_AT) and LEAST > 2
        y_bank = [bank[2], bank[3]]
        h_bank = bank[4:8]
        out_filled = 16 * (1 + GROUPS)

        PEEL = 4

        def plan_of(eng, e):
            return (eng.value_load(plan[0:1, bass.ds(e, 1)], min_val=LEAST, max_val=BLOCKS),
                    eng.value_load(plan[0:1, bass.ds(e + E, 1)], min_val=0, max_val=E * BLOCKS))

        def all_blocks(eng):
            return eng.value_load(plan[0:1, 2 * E:2 * E + 1], min_val=E * LEAST, max_val=E * BLOCKS)

        block = ctx.enter_context(nc.Block())

        @block.sync
        def _(sp):
            sp.dma_start(cond_sb[:, :], cond).then_inc(const_in, 16)
            sp.dma_start(ident_sb[:, :], ident).then_inc(const_in, 16)
            sp.dma_start(w_sb[:, :, :], w.rearrange("(k p) o -> p k o", p=P)).then_inc(const_in, 16)
            sp.dma_start(x_sb[1][:, :, :], x_rows[1, :, :, :]).then_inc(x_loaded[1], 16)
            sp.dma_start(table, empty_table).then_inc(table_empty, 16)
            sp.wait_ge(set_dve, 1)
            sp.dma_start(hidden[T:T + P, :], zero_sb[:, :]).then_inc(pad_zero, 16)
            sp.dma_start(out[T:T + P, :], zero_sb[:, :]).then_inc(out_written, 16)

            def load_weights(e):
                sp.dma_start(w_raw[:, 0:WCOLS].rearrange("p (k f) -> p k f", k=KC),
                             w1_rows[e, :, :, :]).then_inc(w_loaded, 16)
                sp.dma_start(w_raw[:, WCOLS:2 * WCOLS].rearrange("p (c d) -> p c d", c=FC),
                             w2_rows[e, :, :, :]).then_inc(w_loaded, 16)

            load_weights(0)

            def stage1(g, u, t, refill=True):
                sp.wait_ge(x_loaded[u], 16 * (t + 1))
                sp.dma_start(out_rows[g, :, :, :], x_sb[u][:, :, :]).then_inc(out_written, 16)
                if refill:
                    sp.wait_ge(out_written, 16 * (g + 2))
                    sp.sem_inc(sp_paced)
                    sp.wait_ge(t_done, g + 1)
                    sp.dma_start(x_sb[u][:, :, :], x_rows[g + 2, :, :, :]).then_inc(x_loaded[u], 16)

            with sp.Fori(0, GROUPS // 2 - 1) as t:
                for u in range(2):
                    stage1(t * 2 + u, u, t)
            for g in range(GROUPS - 2, GROUPS):
                stage1(g, g % 2, g // 2, refill=False)

            for u in range(2):
                sp.wait_ge(scattered[u], 16 * 2 * TILES * (GROUPS // 2))
            sp.wait_ge(plan_ready, 1)
            with sp.Fori(0, E) as e:
                sp.wait_ge(w_lo_done, PIECES * (e + 1))
                load_weights((e + 1) % E)
                n_blocks, before_e = plan_of(sp, e)
                with sp.Fori(0, n_blocks) as j:
                    sp.wait_ge(t_done, before_e + j + GROUPS)
                    sp.dma_start(gather_ids[:, :, :], table_rows[e * BLOCKS + j, :, :, :]).then_inc(gather_listed, 16)
            n_all = all_blocks(sp)
            for i in range(AHEAD):
                sp.wait_ge(t_done, n_all + (GROUPS + i))
                if i == 0:
                    sp.dma_start(gather_ids[:, :, :], table_rows[E * BLOCKS, :, :, :]).then_inc(gather_listed, 16)
            sp.dma_start(gather_ids[:, :, :], table_rows[E * BLOCKS + 1, :, :, :]).then_inc(gather_listed, 16)
            sp.wait_ge(added, n_all * (16 * SUBS))
            sp.sem_inc(sp_paced)
            sp.wait_ge(w_loaded, 32 * (E + 1))
            sp.wait_ge(gathered, n_all * (16 * SUBS) + 16 * SUBS * AHEAD)
            sp.sem_inc(sp_paced)

        @block.gpsimd
        def _(pool):
            pool.wait_ge(table_empty, 16)

            def scatter(g, u, t):
                pool.wait_ge(pay_ready, g + 1)
                pool.sem_inc(pool_paced)
                for j in range(TILES):
                    for c in range(TOP_K):
                        pool.indirect_dma_start(
                            table, bass.IndirectOffsetOnAxis(slots[u][:, c, j:j + 1], axis=0),
                            pay[u][:, c, j, :], None, bounds_check=TABLE - 1, oob_is_err=False,
                        ).then_inc(scattered[u], 16)

            with pool.Fori(0, GROUPS // 2) as t:
                for u in range(2):
                    scatter(t * 2 + u, u, t)

            def gather():
                for s in range(SUBS):
                    pool.indirect_dma_start(
                        xg[:, s, :], None, hidden,
                        bass.IndirectOffsetOnAxis(gather_ids[:, s, 0:1], axis=0),
                    ).then_inc(gathered, 16)

            pool.wait_ge(pad_zero, 16)
            for u in range(2):
                pool.wait_ge(hid_stored[u], 16 * (GROUPS // 2))
            pool.sem_inc(y_free, SUBS)
            for b in range(AHEAD):
                pool.wait_ge(gather_listed, 16 * (b + 1))
                pool.wait_ge(t_done, GROUPS + b)
                gather()
            pool.wait_ge(out_written, out_filled)
            pool.wait_ge(plan_ready, 1)
            n_all = all_blocks(pool)
            with pool.Fori(0, n_all) as b:
                pool.wait_ge(gather_listed, 16 * (b + 3))
                pool.wait_ge(t_done, b + (GROUPS + 2))
                pool.sem_inc(pool_paced)
                gather()
                pool.wait_ge(add_listed, 16 * (b + 1))
                for s in range(SUBS):
                    pool.wait_ge(y_ready, b * SUBS + (s + 1))
                    pool.sem_inc(pool_paced)
                    pool.indirect_dma_start(
                        out, bass.IndirectOffsetOnAxis(add_ids[:, s, 0:1], axis=0),
                        y_sb[s][:, :], None, compute_op=ALU.add,
                    ).then_inc(added, 16)
                    pool.wait_ge(added, b * (16 * SUBS) + 16 * (s + 1))
                    pool.sem_inc(y_free)

        @block.tensor
        def _(pe):
            def transpose_x(u, count):
                pe.wait_ge(x_loaded[u], count)
                for k in range(KC):
                    for j in range(TILES):
                        mm = pe.transpose(bank[k][:, j * P:(j + 1) * P], x_sb[u][:, j, k * P:(k + 1) * P],
                                          ident_sb[:, :])
                mm.then_inc(t_done, 1)

            pe.wait_ge(const_in, 16 * CONSTS)
            for k in range(KC):
                last = pe.transpose(bank[7][:, k * P:(k + 1) * P], cond_sb[:, k * P:(k + 1) * P], ident_sb[:, :])
            last.then_inc(set_pe, 1)
            transpose_x(0, 16)
            pe.wait_ge(set_dve, 6)
            for o in range(KC):
                for k in range(KC):
                    last = pe.matmul(bank[6][:, o * B:(o + 1) * B], wsq_sb[:, k, o * P:(o + 1) * P],
                                     ysq_t[:, k, :], start=(k == 0), stop=(k == KC - 1))
            last.then_inc(set_pe, 1)

            def positions(g):
                pe.wait_ge(mask_ready, g + 1)
                pe.matmul(bank[7][:, 0:TILES * E], tri_sb[:, :], mask[:, :, :].rearrange("p j e -> p (j e)"),
                          start=True, stop=False)
                pe.matmul(bank[7][:, 0:TILES * E], ones_sb[:, :],
                          before[:, 0:TILES, :].rearrange("p j e -> p (j e)"),
                          start=False, stop=True).then_inc(pos_done, 1)

            def stage1(g, u, t, more=True):
                pe.wait_ge(xs_ready, KC * (g + 1))
                for o in range(KC):
                    for k in range(KC):
                        mm = pe.matmul(bank[2 + o][:, :], w_sb[:, k, o * P:(o + 1) * P], xs_t[:, k, :],
                                       start=(k == 0), stop=(k == KC - 1))
                    mm.then_inc(m_done, 1)
                if not (isinstance(g, int) and g == 0):
                    positions(g - 1)
                if more:
                    transpose_x(1 - u, 16 * (t + u + 1))
                pe.wait_ge(hid_ready, KC * (g + 1))
                for j in range(TILES):
                    for k in range(KC):
                        mm = pe.matmul(bank[6][:, j * E:(j + 1) * E], hid_t[:, k, j * P:(j + 1) * P],
                                       wr_sb[:, k, :], start=(k == 0), stop=(k == KC - 1))
                mm.then_inc(l_done, 1)
                if not (isinstance(g, int) and g == 0):
                    pe.wait_ge(hid_copied, 2 * g)
                for j in range(TILES):
                    for k in range(KC):
                        mm = pe.transpose(bank[4 + j // 2][:, (j % 2) * D + k * P:(j % 2) * D + (k + 1) * P],
                                          hid_t[:, k, j * P:(j + 1) * P], ident_sb[:, :])
                mm.then_inc(back_done, 1)

            for g in range(2):
                stage1(g, g, 0)
            with pe.Fori(1, GROUPS // 2 - 1) as t:
                for u in range(2):
                    stage1(t * 2 + u, u, t)
            for g in range(GROUPS - 2, GROUPS):
                stage1(g, g % 2, g // 2, more=(g < GROUPS - 1))
            positions(GROUPS - 1)
            pe.matmul(bank[6][:, 0:E], ones_sb[:, :], before[:, TILES, :], start=True, stop=True)\
                .then_inc(totals_done, 1)

            def transpose_block(b):
                pe.wait_ge(gathered, b * (16 * SUBS) + 16 * SUBS)
                for k in range(KC):
                    for s in range(SUBS):
                        mm = pe.transpose(bank[0][:, k * SLOTS + s * P:k * SLOTS + (s + 1) * P],
                                          xg[:, s, k * P:(k + 1) * P], ident_sb[:, :])
                mm.then_inc(t_done, 1)

            def first_product(u, f, at):
                h = h_bank[f % RING][:, 0:SLOTS]
                for k in range(KC):
                    cols = slice(k * F + f * P, k * F + (f + 1) * P)
                    hi = xt_hi[:, bass.ds(at + k * SLOTS, SLOTS)]
                    lo = xt_lo[:, bass.ds(at + k * SLOTS, SLOTS)]
                    pe.matmul(h, w_hi[u][:, cols], hi, start=(k == 0), stop=False)
                    pe.matmul(h, w_hi[u][:, cols], lo, start=False, stop=False)
                    mm = pe.matmul(h, w_lo[u][:, cols], hi, start=False, stop=(k == KC - 1))
                mm.then_inc(s1_done, 1)

            def second_product(u, f):
                cols = slice(WCOLS + f * D, WCOLS + (f + 1) * D)
                for s in range(SUBS):
                    hi = h_hi[f % RING][:, s * P:(s + 1) * P]
                    lo = h_lo[f % RING][:, s * P:(s + 1) * P]
                    y = y_bank[s][:, 0:D]
                    pe.matmul(y, hi, w_hi[u][:, cols], start=(f == 0), stop=False)
                    pe.matmul(y, hi, w_lo[u][:, cols], start=False, stop=False)
                    mm = pe.matmul(y, lo, w_hi[u][:, cols], start=False, stop=(f == FC - 1))
                    if f == FC - 1:
                        mm.then_inc(y_done, 1)
                if f < FC - 1:
                    mm.then_inc(s2_done, 1)

            transpose_block(0)
            pe.wait_ge(plan_ready, 1)
            with pe.Fori(0, E // 2) as pair:
                for u in range(2):
                    n_blocks, before_e = plan_of(pe, pair * 2 + u)
                    with pe.Fori(0, n_blocks) as j:
                        b = before_e + j
                        at = (b % 2) * XT
                        pe.wait_ge(w_lo_done, PIECES * (pair * 2 + u + 1))
                        pe.wait_ge(xt_ready, b + 1)
                        for f in range(FC + LAG):
                            if f < FC:
                                if f >= RING:
                                    pe.wait_ge(gelu_done, b * FC + (f + 1 - RING))
                                first_product(u, f, at)
                            if f == 4:
                                transpose_block(b + 1)
                            if f >= LAG:
                                pe.wait_ge(h_ready, b * FC + (f + 1 - LAG))
                                second_product(u, f - LAG)

        @block.scalar
        def _(act):
            act.dma_start(x_sb[0][:, :, :], x_rows[0, :, :, :]).then_inc(x_loaded[0], 16)
            for tile, src in ((tri_f, tri), (low_sb, expert_low), (base_sb, slot_base), (ids_sb, token_ids),
                              (plan_sb, plan_consts), (b1_sb, b1_t),
                              (b2_sb, b2.rearrange("e d -> (e d)").partition_broadcast(P))):
                act.dma_start(tile[:, :], src).then_inc(const_in, 16)
            act.dma_start(wr_sb[:, :, :], wr_t.rearrange("(k p) e -> p k e", p=P)).then_inc(const_in, 16)
            act.wait_ge(set_dve, 7)
            act.activation(root_t[:, :], var_t[:, :], ACT.Sqrt).then_inc(set_act, 1)

            def split_piece(u, i, n_loaded):
                if i == 0:
                    act.wait_ge(w_loaded, n_loaded)
                cols = slice(i * PIECE, (i + 1) * PIECE)
                act.copy(w_hi[u][:, cols], w_raw[:, cols]).then_inc(w_hi_done, 1)

            for i in range(PIECES):
                split_piece(0, i, 32)

            def stage1(g, u, t):
                act.wait_ge(back_done, g + 1)
                if not (isinstance(t, int) and t == 0):
                    act.wait_ge(hid_stored[u], 16 * t)
                for h in range(2):
                    act.copy(hid_sb[u][:, 2 * h:2 * h + 2, :].rearrange("p j d -> p (j d)"),
                             bank[4 + h][:, :]).then_inc(hid_copied, 1)
                act.wait_ge(hid_copied, 2 * (g + 1))
                act.dma_start(hidden_rows[g, :, :, :], hid_sb[u][:, :, :]).then_inc(hid_stored[u], 16)
                act.wait_ge(gap_ready, g + 1)
                act.activation(ratio[:, :], gap[:, :], ACT.Exp).then_inc(ratio_ready, 1)

            for g in range(2):
                stage1(g, g, 0)
            with act.Fori(1, GROUPS // 2) as t:
                for u in range(2):
                    stage1(t * 2 + u, u, t)

            def split_rows(b):
                act.copy(xt_hi[:, bass.ds((b % 2) * XT, XT)], bank[0][:, :]).then_inc(xt_hi_done, 1)

            act.activation(warm_sb[:, :], zero_sb[:, 0:1], ACT.Gelu_apprx_tanh)
            act.wait_ge(t_done, GROUPS + 1)
            split_rows(0)
            act.wait_ge(plan_ready, 1)

            def one_block(u, e, j, b, piece0):
                for f in range(FC):
                    act.wait_ge(s1_done, b * FC + (f + 1))
                    if f >= RING:
                        act.wait_ge(h_ready, b * FC + (f + 1 - RING))
                    if f == 6:
                        act.wait_ge(t_done, b + (GROUPS + 2))
                    act.activation(h_raw[f % RING][:, :], h_bank[f % RING][:, 0:SLOTS], ACT.Gelu_apprx_tanh,
                                   bias=b1_now[u][:, f:f + 1]).then_inc(gelu_done, 1)
                    if f == 5:
                        act.wait_ge(y_free, b * SUBS + SUBS)
                        act.dma_start(add_ids[:, :, :], table_rows[e * BLOCKS + j, :, :, :]).then_inc(add_listed, 16)
                    if f == 6:
                        split_rows(b + 1)
                    if piece0 is not None and f in SPLIT_AT:
                        split_piece(1 - u, piece0 + SPLIT_AT.index(f), 32 * (e + 2))

            with act.Fori(0, E // 2) as pair:
                for u in range(2):
                    e = pair * 2 + u
                    act.copy(b1_now[u][:, :], b1_sb[:, bass.ds(e * FC, FC)]).then_inc(bias_now, 1)
                    act.wait_ge(bias_now, e + 1)
                    n_blocks, before_e = plan_of(act, e)
                    for j in range(2):
                        one_block(u, e, j, before_e + j, j * len(SPLIT_AT))
                    with act.Fori(2, n_blocks) as j:
                        one_block(u, e, j, before_e + j, None)

        @block.vector
        def _(dve):
            dve.memset(zero_sb[:, :], 0.0).then_inc(set_dve, 1)
            dve.memset(ones_sb[:, :], 1.0)
            dve.memset(before[:, :, :], 0.0)
            dve.wait_ge(const_in, 16 * CONSTS)
            dve.tensor_copy(tri_sb[:, :], tri_f[:, :])
            scale = 1.0 / float(np.sqrt(np.float32(D)))
            dve.tensor_tensor(wsq_sb[:, :, :], w_sb[:, :, :], w_sb[:, :, :], ALU.mult).then_inc(set_dve, 1)
            dve.wait_ge(set_pe, 1)
            ys_flat = ys_t[:, :, :].rearrange("p k b -> p (k b)")
            ysq_flat = ysq_t[:, :, :].rearrange("p k b -> p (k b)")
            d_flat = d_t[:, :, :].rearrange("p k b -> p (k b)")
            dve.tensor_scalar(ys_flat, bank[7][:, 0:KC * B], scale, None, ALU.mult).then_inc(set_dve, 1)
            dve.wait_ge(set_dve, 3)
            dve.tensor_tensor(ysq_flat, ys_flat, ys_flat, ALU.mult).then_inc(set_dve, 3)
            dve.wait_ge(set_pe, 2)
            dve.tensor_scalar(var_t[:, :], bank[6][:, 0:KC * B], EPS, None, ALU.add).then_inc(set_dve, 1)
            dve.wait_ge(set_act, 1)
            dve.reciprocal(root_t[:, :], root_t[:, :]).then_inc(set_dve, 1)
            dve.wait_ge(set_dve, 8)
            dve.tensor_tensor(tmp_t[:, :], root_t[:, :], root_t[:, :], ALU.mult).then_inc(set_dve, 1)
            dve.wait_ge(set_dve, 9)
            dve.tensor_tensor(tmp_t[:, :], tmp_t[:, :], var_t[:, :], ALU.mult).then_inc(set_dve, 1)
            dve.wait_ge(set_dve, 10)
            dve.tensor_scalar(tmp_t[:, :], tmp_t[:, :], -0.5, 1.5, ALU.mult, ALU.add).then_inc(set_dve, 1)
            dve.wait_ge(set_dve, 11)
            dve.tensor_tensor(d_flat, tmp_t[:, :], root_t[:, :], ALU.mult).then_inc(set_dve, 1)
            dve.wait_ge(set_dve, 12)

            def split_piece(u, i, count):
                cols = slice(i * PIECE, (i + 1) * PIECE)
                dve.wait_ge(w_hi_done, count)
                dve.tensor_tensor(w_lo[u][:, cols], w_raw[:, cols], w_hi[u][:, cols].bitcast(F32),
                                  ALU.subtract).then_inc(w_lo_done, 1)

            def by_batch(tile, k, g):
                return tile[:, k, bass.ds(g * GB, GB)].unsqueeze(2).to_broadcast([P, GB, S])

            def scale_x(g):
                dve.wait_ge(t_done, g + 1)
                for k in range(KC):
                    dve.tensor_tensor(xs_t[:, k, :].rearrange("p (b s) -> p b s", s=S),
                                      bank[k][:, :].rearrange("p (b s) -> p b s", s=S),
                                      by_batch(ys_t, k, g), ALU.mult).then_inc(xs_ready, 1)

            scale_x(0)
            for i in range(PIECES):
                split_piece(0, i, i + 1)

            STEPS_A, STEPS_B = 13, 3

            low3 = low_sb[:, :].unsqueeze(1).to_broadcast(RE)
            base3 = base_sb[:, :].unsqueeze(1).to_broadcast(RE)

            def over_e(a):
                return a.unsqueeze(2).to_broadcast(RE)

            def stepper(start):
                n = [0]

                def then(ins):
                    n[0] += 1
                    ins.then_inc(step, 1)
                    dve.wait_ge(step, start + n[0])
                return n, then

            def scale_hidden(g):
                for o in range(KC):
                    dve.wait_ge(m_done, KC * g + (o + 1))
                    dve.tensor_tensor(hid_t[:, o, :].rearrange("p (b s) -> p b s", s=S),
                                      bank[2 + o][:, :].rearrange("p (b s) -> p b s", s=S),
                                      by_batch(d_t, o, g), ALU.mult).then_inc(hid_ready, 1)

            def choose_experts(g):
                n, then = stepper(g * (STEPS_A + STEPS_B))
                dve.wait_ge(l_done, g + 1)
                then(dve.tensor_copy(logits[:, :, :].rearrange("p j e -> p (j e)"), bank[6][:, 0:TILES * E]))

                def choose(c, values, one_hot):
                    then(dve.tensor_reduce(top[:, c, :], values, AX_X, ALU.max))
                    then(dve.tensor_tensor(hit[:, :, :], values, over_e(top[:, c, :]), ALU.is_equal))
                    then(dve.tensor_tensor(hit[:, :, :], hit[:, :, :], low3, ALU.mult))
                    then(dve.tensor_reduce(low[:, c, :], hit[:, :, :], AX_X, ALU.min))
                    return dve.tensor_tensor(one_hot, low3, over_e(low[:, c, :]), ALU.is_equal)

                then(choose(0, logits[:, :, :], first[:, :, :]))
                then(dve.scalar_tensor_tensor(rest[:, :, :], first[:, :, :], -BIG, logits[:, :, :],
                                              ALU.mult, ALU.add))
                ins = choose(1, rest[:, :, :], second[:, :, :])
                dve.tensor_tensor(gap[:, :], top[:, 1, :], top[:, 0, :], ALU.subtract).then_inc(gap_ready, 1)
                then(ins)
                then(dve.tensor_tensor(mask[:, :, :], first[:, :, :], second[:, :, :], ALU.add))
                for j in range(TILES):
                    ins = dve.tensor_tensor(before[:, j + 1, :], before[:, j, :], mask[:, j, :], ALU.add)
                    if j < TILES - 1:
                        ins.then_inc(chain, 1)
                        dve.wait_ge(chain, g * (TILES - 1) + (j + 1))
                ins.then_inc(mask_ready, 1)
                assert n[0] == STEPS_A, n[0]

            def list_pairs(g, u, t):
                n, then = stepper(g * (STEPS_A + STEPS_B) + STEPS_A)
                dve.wait_ge(pos_done, g + 1)
                pos = bank[7][:, 0:TILES * E].rearrange("p (j e) -> p j e", e=E)
                dve.tensor_scalar(over[:, :, :], pos, float(CAP), NO_SLOT, ALU.is_gt, ALU.mult)
                dve.tensor_tensor(slot_e[:, :, :], pos, base3, ALU.add)
                dve.tensor_copy(before[:, 0, :], before[:, TILES, :])
                dve.wait_ge(ratio_ready, g + 1)
                then(dve.tensor_scalar(total[:, :], ratio[:, :], 1.0, None, ALU.add))
                dve.tensor_tensor(slot_e[:, :, :], slot_e[:, :, :], over[:, :, :], ALU.add)
                then(dve.reciprocal(total[:, :], total[:, :]))
                if not (isinstance(t, int) and t == 0):
                    dve.wait_ge(scattered[u], (16 * TOP_K * TILES) * t)
                gates = pay[u].bitcast(F32)
                dve.tensor_tensor(hit[:, :, :], first[:, :, :], slot_e[:, :, :], ALU.mult)
                dve.tensor_tensor(rest[:, :, :], second[:, :, :], slot_e[:, :, :], ALU.mult)
                dve.tensor_copy(gates[:, 0, :, 1], total[:, :])
                then(dve.tensor_tensor(gates[:, 1, :, 1], total[:, :], ratio[:, :], ALU.mult))
                for c in range(TOP_K):
                    dve.tensor_copy(pay[u][:, c, :, 0], ids_sb[:, bass.ds(g * TILES, TILES)])
                with nc.allow_low_precision(reason="whole numbers below 2**24"):
                    dve.tensor_reduce(slots[u][:, 0, :], hit[:, :, :], AX_X, ALU.add)
                    dve.tensor_reduce(slots[u][:, 1, :], rest[:, :, :], AX_X, ALU.add).then_inc(pay_ready, 1)
                assert n[0] == STEPS_B, n[0]

            def stage1(g, u, t, more=True):
                scale_hidden(g)
                if more:
                    scale_x(g + 1)
                if not (isinstance(g, int) and g == 0):
                    list_pairs(g - 1, 1 - u, t - 1 + u)
                choose_experts(g)

            for g in range(PEEL):
                stage1(g, g % 2, g // 2)
            with dve.Fori(PEEL // 2, GROUPS // 2 - 1) as t:
                for u in range(2):
                    stage1(t * 2 + u, u, t)
            for g in range(GROUPS - 2, GROUPS):
                stage1(g, g % 2, g // 2, more=(g < GROUPS - 1))
            list_pairs(GROUPS - 1, (GROUPS - 1) % 2, (GROUPS - 1) // 2)

            dve.wait_ge(totals_done, 1)
            dve.tensor_tensor(steps_e[:, :, :], bank[6][:, 0:E].unsqueeze(2).to_broadcast([P, E, BLOCKS]),
                              plan_sb[:, 0:BLOCKS].unsqueeze(1).to_broadcast([P, E, BLOCKS]),
                              ALU.is_gt).then_inc(plan_step, 1)
            dve.wait_ge(plan_step, 1)
            dve.tensor_reduce(count_e[:, :], steps_e[:, :, :], AX_X, ALU.add).then_inc(plan_step, 1)
            dve.wait_ge(plan_step, 2)
            dve.tensor_scalar(count_e[:, :], count_e[:, :], float(LEAST), None, ALU.max).then_inc(plan_step, 1)
            dve.wait_ge(plan_step, 3)
            dve.tensor_tensor(sums_e[:, :, :], count_e[:, :].unsqueeze(1).to_broadcast([P, E + 1, E]),
                              plan_sb[:, BLOCKS:].rearrange("p (a e) -> p a e", e=E),
                              ALU.mult).then_inc(plan_step, 1)
            dve.tensor_copy(plan[:, 0:E], count_e[:, :])
            dve.wait_ge(plan_step, 4)
            with nc.allow_low_precision(reason="whole numbers below 2**24"):
                dve.tensor_reduce(plan[:, E:2 * E + 1], sums_e[:, :, :], AX_X, ALU.add).then_inc(plan_ready, 1)

            def split_rows(b):
                dve.wait_ge(xt_hi_done, b + 1)
                cols = bass.ds((b % 2) * XT, XT)
                dve.tensor_tensor(xt_lo[:, cols], bank[0][:, :], xt_hi[:, cols].bitcast(F32),
                                  ALU.subtract).then_inc(xt_ready, 1)

            split_rows(0)
            dve.wait_ge(plan_ready, 1)

            def one_block(u, e, b, piece0):
                for f in range(FC):
                    dve.wait_ge(gelu_done, b * FC + (f + 1))
                    if f >= RING:
                        dve.wait_ge(s2_done, b * (FC - 1) + (f + 1 - RING))
                    dve.tensor_copy(h_hi[f % RING][:, :], h_raw[f % RING][:, :]).then_inc(hi_done, 1)
                    dve.wait_ge(hi_done, b * FC + (f + 1))
                    dve.tensor_tensor(h_lo[f % RING][:, :], h_raw[f % RING][:, :],
                                      h_hi[f % RING][:, :].bitcast(F32), ALU.subtract).then_inc(h_ready, 1)
                    if piece0 is not None and f in SPLIT_AT:
                        i = piece0 + SPLIT_AT.index(f)
                        split_piece(1 - u, i, PIECES * (e + 1) + (i + 1))
                    if f == 6:
                        split_rows(b + 1)
                for s in range(SUBS):
                    dve.wait_ge(y_done, b * SUBS + (s + 1))
                    dve.wait_ge(y_free, b * SUBS + (s + 1))
                    dve.tensor_tensor(y_sb[s][:, :], y_bank[s][:, 0:D], b2_sb[:, bass.ds(e * D, D)],
                                      ALU.add).then_inc(y_biased, 1)
                dve.wait_ge(add_listed, 16 * (b + 1))
                for s in range(SUBS):
                    dve.wait_ge(y_biased, b * SUBS + (s + 1))
                    dve.tensor_scalar(y_sb[s][:, :], y_sb[s][:, :], add_ids.bitcast(F32)[:, s, 1:2],
                                      None, ALU.mult).then_inc(y_ready, 1)

            with dve.Fori(0, E // 2) as pair:
                for u in range(2):
                    e = pair * 2 + u
                    n_blocks, before_e = plan_of(dve, e)
                    for j in range(2):
                        one_block(u, e, before_e + j, j * len(SPLIT_AT))
                    with dve.Fori(2, n_blocks) as j:
                        one_block(u, e, before_e + j, None)


def constants():
    p = np.arange(P)
    empty = np.zeros((TABLE, 2), np.int32)
    empty[:, 0] = T + (np.arange(TABLE) % SLOTS) // SUBS
    more_than = np.arange(BLOCKS) * SLOTS
    earlier = np.arange(E)[None, :] < np.arange(E + 1)[:, None]
    return {
        "ident": np.eye(P, dtype=np.float32),
        "tri": (p[:, None] <= p[None, :]).astype(np.float32),
        "expert_low": np.tile(np.arange(E, dtype=np.float32) - E, (P, 1)),
        "slot_base": np.tile(np.arange(E, dtype=np.float32) * CAP - 1, (P, 1)),
        "token_ids": (np.arange(T // P, dtype=np.int32)[None, :] * P + p[:, None].astype(np.int32)),
        "plan_consts": np.tile(np.concatenate([more_than, earlier.ravel()]).astype(np.float32), (P, 1)),
        "empty_table": empty,
    }


def kernel(x, cond_1024, L0_cond_weight, L0_ffn_wr, L0_ffn_w1, L0_ffn_b1, L0_ffn_w2, L0_ffn_b2):
    import concourse.bacc as bacc
    from concourse.bass_utils import run_bass_kernel_spmd

    arrays = {
        "x": x,
        "cond": cond_1024,
        "w": L0_cond_weight,
        "wr_t": np.asarray(L0_ffn_wr).T,
        "w1": L0_ffn_w1,
        "b1_t": np.asarray(L0_ffn_b1).reshape(E, FC, P).transpose(2, 0, 1).reshape(P, E * FC),
        "w2": L0_ffn_w2,
        "b2": L0_ffn_b2,
        **constants(),
    }
    arrays = {f"in_{k}": np.ascontiguousarray(v) for k, v in arrays.items()}
    nc = bacc.Bacc("TRN2", target_bir_lowering=False, num_devices=1)
    args = [nc.dram_tensor(k, v.shape, mybir.dt.from_np(v.dtype), kind="ExternalInput").ap()
            for k, v in arrays.items()]
    out = nc.dram_tensor("out_rows", (T + P, D), F32, kind="ExternalOutput").ap()
    build(nc, *args, out)
    r = run_bass_kernel_spmd(nc, [arrays], core_ids=[0])
    return r.results[0]["out_rows"][:T].reshape(B, S, D)
```

```python
from contextlib import ExitStack

import numpy as np

import concourse.bass as bass
from concourse import mybir

F32 = mybir.dt.float32
F32R = mybir.dt.float32r
BF16 = mybir.dt.bfloat16
I32 = mybir.dt.int32
ALU = mybir.AluOpType
ACT = mybir.ActivationFunctionType
AX_X = mybir.AxisListType.X

P = 128
B, S, D = 128, 64, 256
E, F, TOP_K = 8, 1024, 2
T = B * S
CAP = max(8, int(max(1, T * TOP_K // E) * 1.25))
KC = D // P
FC = F // P
EPS = 1e-8

TILES = 4
ROWS = TILES * P
GROUPS = T // ROWS
GB = ROWS // S
SUBS = 2
SLOTS = SUBS * P
BLOCKS = CAP // SLOTS
LEAST = 4
LAG = 3
TILES_E = CAP // P
COLS = E * TILES_E + SUBS
TABLE = P * COLS
RING = 4
OPEN = 2
assert CAP % SLOTS == 0 and ROWS == 512 and T % (4 * ROWS) == 0

WCOLS = KC * F
PIECE = 512
PIECES = 2 * WCOLS // PIECE
PAD = SUBS * P
NO_SLOT = float(1 << 22)
BIG = 3.0e38


def build(nc, x, cond, w, wr_t, w1, b1_t, w2, b2, ident, tri, expert_low, slot_base, token_ids,
          plan_consts, empty_table, out):
    hidden = nc.dram_tensor("hidden", [T + PAD, D], F32, kind="Internal").ap()
    table = nc.dram_tensor("table", [TABLE, 2], I32, kind="Internal").ap()

    x_rows = x.rearrange("b s d -> (b s) d").rearrange("(g j p) d -> g p j d", j=TILES, p=P)
    out_rows = out[0:T, :].rearrange("(g j p) d -> g p j d", j=TILES, p=P)
    hidden_rows = hidden[0:T, :].rearrange("(g j p) d -> g p j d", j=TILES, p=P)
    table_rows = table.rearrange("(p c) v -> p c v", p=P)
    w1_rows = w1.rearrange("e (k p) f -> e p k f", p=P)
    w2_rows = w2.rearrange("e (c p) d -> e p c d", p=P)

    with ExitStack() as ctx:
        def sb(name, shape, dt=F32):
            return ctx.enter_context(nc.sbuf_tensor("sb_" + name, shape, dt))

        def sem(name):
            return ctx.enter_context(nc.semaphore(name))

        bank = [ctx.enter_context(nc.psum_tensor(f"bank{i}", [P, 512], F32)) for i in range(8)]

        ident_sb = sb("ident", [P, P])
        tri_f = sb("tri_f", [P, P])
        tri_sb = sb("tri", [P, P], BF16)
        ones_sb = sb("ones", [P, P], BF16)
        low_sb = sb("expert_low", [P, E])
        base_sb = sb("slot_base", [P, E])
        ids_sb = sb("ids", [P, T // P], I32)
        cond_sb = sb("cond", [P, D])
        w_sb = sb("w", [P, KC, D])
        wsq_sb = sb("wsq", [P, KC, D])
        wr_sb = sb("wr", [P, KC, E])
        b1_sb = sb("b1", [P, E * FC])
        b2_sb = sb("b2", [P, E * D])
        warm_sb = sb("warm", [P, 1])
        b1_now = [sb(f"b1_now{u}", [P, FC]) for u in range(2)]
        zero_sb = sb("zero", [P, D])
        plan_sb = sb("plan_consts", [P, BLOCKS + (E + 1) * E])
        steps_e = sb("steps_e", [P, E, BLOCKS])
        count_e = sb("count_e", [P, E + 1])
        sums_e = sb("sums_e", [P, E + 1, E])
        before_e = sb("before_e", [P, E + 1])
        plan_f = sb("plan_f", [P, E + 1])
        plan = sb("plan", [P, 2 * (E + 1)], I32)
        ys_t = sb("ys_t", [P, KC, B])
        ysq_t = sb("ysq_t", [P, KC, B])
        var_t = sb("var_t", [P, KC * B])
        root_t = sb("root_t", [P, KC * B])
        tmp_t = sb("tmp_t", [P, KC * B])
        d_t = sb("d_t", [P, KC, B])

        x_sb = [sb(f"x{u}", [P, TILES, D]) for u in range(2)]
        xs_t = sb("xs_t", [P, KC, ROWS])
        hid_t = sb("hid_t", [P, KC, ROWS])
        hid_sb = [sb(f"hid{u}", [P, TILES, D]) for u in range(2)]
        RE = [P, TILES, E]
        logits = sb("logits", RE)
        rest = sb("rest", RE)
        hit = sb("hit", RE)
        first = sb("first", RE)
        second = sb("second", RE)
        mask = sb("mask", RE, BF16)
        of_group = sb("of_group", [P, E], BF16)
        before = sb("before", [P, E], BF16)
        slot_e = sb("slot_e", RE)
        over = sb("over", RE)
        top = sb("top", [P, 2, TILES])
        low = sb("low", [P, 2, TILES])
        gap = sb("gap", [P, TILES])
        ratio = sb("ratio", [P, TILES])
        total = sb("total", [P, TILES])
        picked = sb("picked", [P, 2, TILES, E])
        slot_of = sb("slot_of", [P, 2, TILES], I32)
        low_bits = sb("low_bits", [P, 2, TILES], I32)
        high_bits = sb("high_bits", [P, 2, TILES], I32)
        slots = [sb(f"slots{u}", [P, 2, TILES], I32) for u in range(2)]
        pay = [sb(f"pay{u}", [P, 2, TILES, 2], I32) for u in range(2)]

        w_raw = sb("w_raw", [P, 2 * WCOLS])
        w_hi = [sb(f"w_hi{u}", [P, 2 * WCOLS], F32R) for u in range(2)]
        w_lo = [sb(f"w_lo{u}", [P, 2 * WCOLS], F32R) for u in range(2)]
        table_sb = sb("table", [P, COLS, 2], I32)
        table_first = sb("table_first", [P, LAG * SUBS, 2], I32)
        filled = sb("filled", [P, 1], I32)
        gather_ids = sb("gather_ids", [P, SUBS], I32)
        add_ids = sb("add_ids", [P, SUBS], I32)
        ids_ring = sb("ids_ring", [P, 4 * SUBS], I32)
        xg_first = sb("xg_first", [P, SUBS, D])
        xg_third = sb("xg_third", [P, SUBS, D])
        xg = sb("xg", [P, SUBS, D])
        XT = KC * SLOTS
        xt_hi = sb("xt_hi", [P, XT], F32R)
        xt_lo = sb("xt_lo", [P, XT], F32R)
        h_raw = [sb(f"h_raw{i}", [P, SLOTS]) for i in range(RING)]
        h_hi = [sb(f"h_hi{i}", [P, SLOTS], F32R) for i in range(RING)]
        h_lo = [sb(f"h_lo{i}", [P, SLOTS], F32R) for i in range(RING)]
        y_sb = [sb(f"y{s}", [P, D]) for s in range(SUBS)]

        first_in = sem("first_in")
        const_in = sem("const_in")
        late_in = sem("late_in")
        table_empty = sem("table_empty")
        pad_zero = sem("pad_zero")
        set_dve = sem("set_dve")
        set_pe = sem("set_pe")
        set_act = sem("set_act")
        w_loaded = sem("w_loaded")
        x_loaded = [sem(f"x_loaded{u}") for u in range(2)]
        hid_stored = [sem(f"hid_stored{u}") for u in range(2)]
        scattered = [sem(f"scattered{u}") for u in range(2)]
        out_written = sem("out_written")
        added = sem("added")
        y_free = sem("y_free")
        t_done = sem("t_done")
        xs_ready = sem("xs_ready")
        m_done = sem("m_done")
        hid_ready = sem("hid_ready")
        l_done = sem("l_done")
        back_done = sem("back_done")
        hid_copied = sem("hid_copied")
        step = sem("step")
        counted = sem("counted")
        mask_ready = sem("mask_ready")
        pos_done = sem("pos_done")
        gap_ready = sem("gap_ready")
        ratio_ready = sem("ratio_ready")
        pay_ready = sem("pay_ready")
        pool_paced = sem("pool_paced")
        sp_paced = sem("sp_paced")
        bias_now = sem("bias_now")
        totals_done = sem("totals_done")
        plan_step = sem("plan_step")
        plan_ready = sem("plan_ready")
        first_loaded = sem("first_loaded")
        filled_ready = sem("filled_ready")
        table_loaded = sem("table_loaded")
        gather_listed = sem("gather_listed")
        add_listed = sem("add_listed")
        gathered_first = sem("gathered_first")
        gathered_third = sem("gathered_third")
        gathered = sem("gathered")
        w_hi_done = sem("w_hi_done")
        w_lo_done = sem("w_lo_done")
        xt_hi_done = sem("xt_hi_done")
        xt_ready = sem("xt_ready")
        xt_used = sem("xt_used")
        h_open = sem("h_open")
        gelu_done = sem("gelu_done")
        h_ready = sem("h_ready")
        y_done = sem("y_done")
        y_biased = sem("y_biased")
        y_ready = sem("y_ready")

        CONSTS = 5
        SPLIT_AT = (2, 3, 4, 5)
        assert PIECES == 2 * len(SPLIT_AT) and LEAST > LAG == 3 and BLOCKS < 16
        y_bank = [bank[2], bank[3]]
        h_bank = bank[4:8]
        out_filled = 16 * (SUBS + GROUPS)

        PEEL = 4
        FILLING = GROUPS - 3

        def plan_of(eng, e):
            both = eng.value_load(plan[0:1, bass.ds(e, 1)], min_val=0)
            before = both // 16
            return before, before + both % 16 + LEAST

        def all_blocks(eng, less=0):
            at = less * (E + 1) + E
            return eng.value_load(plan[0:1, at:at + 1], min_val=16 * (E * LEAST - less * LAG)) // 16

        block = ctx.enter_context(nc.Block())

        @block.sync
        def _(sp):
            sp.dma_start(cond_sb[:, :], cond).then_inc(first_in, 16)
            sp.dma_start(ident_sb[:, :], ident).then_inc(first_in, 16)
            sp.dma_start(w_sb[:, :, :], w.rearrange("(k p) o -> p k o", p=P)).then_inc(first_in, 16)
            sp.dma_start(x_sb[1][:, :, :], x_rows[1, :, :, :]).then_inc(x_loaded[1], 16)
            sp.dma_start(table, empty_table).then_inc(table_empty, 16)
            sp.wait_ge(set_dve, 1)
            for s in range(SUBS):
                rows = slice(T + s * P, T + (s + 1) * P)
                sp.dma_start(hidden[rows, :], zero_sb[:, :]).then_inc(pad_zero, 16)
                sp.dma_start(out[rows, :], zero_sb[:, :]).then_inc(out_written, 16)

            def load_weights(e):
                sp.dma_start(w_raw[:, 0:WCOLS].rearrange("p (k f) -> p k f", k=KC),
                             w1_rows[e, :, :, :]).then_inc(w_loaded, 16)
                sp.dma_start(w_raw[:, WCOLS:2 * WCOLS].rearrange("p (c d) -> p c d", c=FC),
                             w2_rows[e, :, :, :]).then_inc(w_loaded, 16)

            load_weights(0)
            for tile, src in ((plan_sb, plan_consts), (b1_sb, b1_t),
                              (b2_sb, b2.rearrange("e d -> (e d)").partition_broadcast(P))):
                sp.dma_start(tile[:, :], src).then_inc(late_in, 16)

            def stage1(g, u, t, refill=True):
                sp.wait_ge(x_loaded[u], 16 * (t + 1))
                sp.dma_start(out_rows[g, :, :, :], x_sb[u][:, :, :]).then_inc(out_written, 16)
                if refill:
                    sp.wait_ge(out_written, 16 * (g + 1 + SUBS))
                    sp.sem_inc(sp_paced)
                    sp.wait_ge(t_done, g + 1)
                    sp.dma_start(x_sb[u][:, :, :], x_rows[g + 2, :, :, :]).then_inc(x_loaded[u], 16)

            with sp.Fori(0, GROUPS // 2 - 1) as t:
                for u in range(2):
                    stage1(t * 2 + u, u, t)
            sp.wait_ge(filled_ready, 1)
            is_filled = sp.value_load(filled[0:1, 0:1], min_val=0, max_val=1)
            with sp.If(is_filled == 1):
                for u in range(2):
                    sp.wait_ge(scattered[u], 16 * TOP_K * TILES * ((FILLING + 1 - u) // 2))
                sp.dma_start(table_first[:, :, :], table_rows[:, 0:LAG * SUBS, :]).then_inc(first_loaded, 16)
            for g in range(GROUPS - 2, GROUPS):
                stage1(g, g % 2, g // 2, refill=False)

            sp.wait_ge(w_lo_done, PIECES)
            load_weights(1)
            for u in range(2):
                sp.wait_ge(scattered[u], 16 * 2 * TILES * (GROUPS // 2))
            sp.dma_start(table_sb[:, :, :], table_rows).then_inc(table_loaded, 16)
            with sp.Fori(1, E) as e:
                sp.wait_ge(w_lo_done, PIECES * (e + 1))
                load_weights((e + 1) % E)
            sp.wait_ge(plan_ready, 1)
            n_all = all_blocks(sp)
            sp.wait_ge(added, n_all * (16 * SUBS))
            sp.sem_inc(sp_paced)
            sp.wait_ge(w_loaded, 32 * (E + 1))
            sp.wait_ge(gathered, n_all * (16 * SUBS))
            sp.sem_inc(sp_paced)

        @block.gpsimd
        def _(pool):
            pool.wait_ge(table_empty, 16)

            def scatter(g, u, t):
                pool.wait_ge(pay_ready, g + 1)
                pool.sem_inc(pool_paced)
                for j in range(TILES):
                    for c in range(TOP_K):
                        pool.indirect_dma_start(
                            table, bass.IndirectOffsetOnAxis(slots[u][:, c, j:j + 1], axis=0),
                            pay[u][:, c, j, :], None, bounds_check=TABLE - 1, oob_is_err=False,
                        ).then_inc(scattered[u], 16)

            def gather(into=xg, block_ids=gather_ids, landed=gathered):
                for s in range(SUBS):
                    pool.indirect_dma_start(
                        into[:, s, :], None, hidden,
                        bass.IndirectOffsetOnAxis(block_ids[:, s:s + 1], axis=0),
                    ).then_inc(landed, 16)

            def list_block(k, tile):
                ids = table_sb[:, bass.ds(tile, SUBS), 0]
                pool.tensor_copy(gather_ids[:, :], ids)
                pool.tensor_copy(ids_ring[:, bass.ds((k % 4) * SUBS, SUBS)], ids).then_inc(gather_listed, 1)

            def first_blocks(source):
                pool.tensor_copy(ids_ring[:, 0:LAG * SUBS], source[:, 0:LAG * SUBS, 0]).then_inc(gather_listed, LAG)
                pool.wait_ge(gather_listed, LAG)
                gather(xg_first, ids_ring, gathered_first)
                gather(xg, ids_ring[:, SUBS:2 * SUBS])
                gather(xg_third, ids_ring[:, 2 * SUBS:], gathered_third)

            with pool.Fori(0, GROUPS // 2 - 1) as t:
                for u in range(2):
                    scatter(t * 2 + u, u, t)
            pool.wait_ge(filled_ready, 1)
            is_filled = pool.value_load(filled[0:1, 0:1], min_val=0, max_val=1)
            with pool.If(is_filled == 1):
                pool.wait_ge(first_loaded, 16)
                for u in range(2):
                    pool.wait_ge(hid_stored[u], 16 * ((FILLING + 1 - u) // 2))
                first_blocks(table_first)
            for g in range(GROUPS - 2, GROUPS):
                scatter(g, g % 2, g // 2)

            def add_tile(b, s):
                pool.indirect_dma_start(
                    out, bass.IndirectOffsetOnAxis(add_ids[:, s:s + 1], axis=0),
                    y_sb[s][:, :], None, compute_op=ALU.add,
                ).then_inc(added, 16)

            def adds_landed(b):
                pool.wait_ge(added, b * (16 * SUBS) + 16 * SUBS)
                pool.sem_inc(y_free, SUBS)

            def begin_adds(b):
                pool.wait_ge(y_ready, b * SUBS + 1)
                pool.sem_inc(pool_paced)
                pool.tensor_copy(add_ids[:, :], ids_ring[:, bass.ds((b % 4) * SUBS, SUBS)]).then_inc(add_listed, 1)
                pool.wait_ge(add_listed, b + 1)
                pool.sem_inc(pool_paced)
                add_tile(b, 0)

            def end_adds(b):
                pool.wait_ge(y_ready, b * SUBS + 2)
                pool.sem_inc(pool_paced)
                add_tile(b, 1)
                adds_landed(b)

            def one_block(b, tile):
                k = b + LAG
                begin_adds(b)
                pool.wait_ge(t_done, GROUPS + k)
                pool.sem_inc(pool_paced)
                list_block(k, tile)
                pool.wait_ge(gather_listed, k + 1)
                pool.sem_inc(pool_paced)
                gather()
                end_adds(b)

            with pool.If(is_filled == 0):
                pool.wait_ge(pad_zero, 16 * SUBS)
                for u in range(2):
                    pool.wait_ge(hid_stored[u], 16 * (GROUPS // 2))
                pool.wait_ge(table_loaded, 16)
                first_blocks(table_sb)
            pool.wait_ge(gathered_third, 16 * SUBS)
            pool.wait_ge(t_done, GROUPS + 2)
            for s in range(SUBS):
                pool.dma_start(xg[:, s, :], xg_third[:, s, :]).then_inc(gathered, 16)
            pool.wait_ge(pad_zero, 16 * SUBS)
            for u in range(2):
                pool.wait_ge(hid_stored[u], 16 * (GROUPS // 2))
            pool.wait_ge(table_loaded, 16)
            pool.sem_inc(y_free, SUBS)
            pool.wait_ge(out_written, out_filled)
            pool.wait_ge(plan_ready, 1)
            _, end = plan_of(pool, 0)
            with pool.Fori(0, end - LAG) as b:
                one_block(b, (b + LAG) * SUBS)
            with pool.Fori(1, E) as e:
                both = pool.value_load(plan[0:1, bass.ds(e + (E + 1), 1)], min_val=0)
                start = both // 16
                with pool.Fori(start, start + both % 16 + LEAST) as b:
                    one_block(b, e * TILES_E + (b - start) * SUBS)
            rest = all_blocks(pool, less=1)
            one_block(rest, E * TILES_E)
            for i in (1, 2):
                begin_adds(rest + i)
                end_adds(rest + i)

        @block.tensor
        def _(pe):
            def transpose_x(u, count):
                pe.wait_ge(x_loaded[u], count)
                for k in range(KC):
                    for j in range(TILES):
                        mm = pe.transpose(bank[k][:, j * P:(j + 1) * P], x_sb[u][:, j, k * P:(k + 1) * P],
                                          ident_sb[:, :])
                mm.then_inc(t_done, 1)

            pe.wait_ge(first_in, 16 * 3)
            for k in range(KC):
                last = pe.transpose(bank[7][:, k * P:(k + 1) * P], cond_sb[:, k * P:(k + 1) * P], ident_sb[:, :])
            last.then_inc(set_pe, 1)
            transpose_x(0, 16)
            pe.wait_ge(set_dve, 6)
            for o in range(KC):
                for k in range(KC):
                    last = pe.matmul(bank[6][:, o * B:(o + 1) * B], wsq_sb[:, k, o * P:(o + 1) * P],
                                     ysq_t[:, k, :], start=(k == 0), stop=(k == KC - 1))
            last.then_inc(set_pe, 1)

            def positions(g):
                pe.wait_ge(mask_ready, g + 1)
                if isinstance(g, int) and g == FILLING:
                    pe.matmul(bank[7][:, TILES * E:TILES * E + 1], ones_sb[:, :], before[:, 0:1],
                              start=True, stop=True)
                pe.matmul(bank[7][:, 0:TILES * E], tri_sb[:, :], mask[:, :, :].rearrange("p j e -> p (j e)"),
                          start=True, stop=False)
                for j in range(1, TILES):
                    pe.matmul(bank[7][:, j * E:TILES * E], ones_sb[:, :],
                              mask[:, 0:TILES - j, :].rearrange("p j e -> p (j e)"), start=False, stop=False)
                pe.matmul(bank[7][:, 0:TILES * E].rearrange("p (j e) -> p j e", e=E), ones_sb[:, :],
                          before[:, :].unsqueeze(1).to_broadcast(RE), start=False, stop=True).then_inc(pos_done, 1)

            def stage1(g, u, t, more=True):
                pe.wait_ge(xs_ready, KC * (g + 1))
                for o in range(KC):
                    for k in range(KC):
                        mm = pe.matmul(bank[2 + o][:, :], w_sb[:, k, o * P:(o + 1) * P], xs_t[:, k, :],
                                       start=(k == 0), stop=(k == KC - 1))
                    mm.then_inc(m_done, 1)
                if not (isinstance(g, int) and g == 0):
                    positions(g - 1)
                if more:
                    transpose_x(1 - u, 16 * (t + u + 1))
                pe.wait_ge(hid_ready, KC * (g + 1))
                for j in range(TILES):
                    for k in range(KC):
                        mm = pe.matmul(bank[6][:, j * E:(j + 1) * E], hid_t[:, k, j * P:(j + 1) * P],
                                       wr_sb[:, k, :], start=(k == 0), stop=(k == KC - 1))
                mm.then_inc(l_done, 1)
                if not (isinstance(g, int) and g == 0):
                    pe.wait_ge(hid_copied, 2 * g)
                for j in range(TILES):
                    for k in range(KC):
                        mm = pe.transpose(bank[4 + j // 2][:, (j % 2) * D + k * P:(j % 2) * D + (k + 1) * P],
                                          hid_t[:, k, j * P:(j + 1) * P], ident_sb[:, :])
                mm.then_inc(back_done, 1)

            for g in range(2):
                stage1(g, g, 0)
            with pe.Fori(1, GROUPS // 2 - 1) as t:
                for u in range(2):
                    stage1(t * 2 + u, u, t)
            for g in range(GROUPS - 2, GROUPS):
                stage1(g, g % 2, g // 2, more=(g < GROUPS - 1))
            positions(GROUPS - 1)
            for j in range(TILES):
                pe.matmul(bank[6][:, 0:E], ones_sb[:, :], mask[:, j, :], start=(j == 0), stop=False)
            pe.matmul(bank[6][:, 0:E], ones_sb[:, :], before[:, :], start=False, stop=True)\
                .then_inc(totals_done, 1)

            def transpose_block(rows=xg):
                for k in range(KC):
                    for s in range(SUBS):
                        mm = pe.transpose(bank[0][:, k * SLOTS + s * P:k * SLOTS + (s + 1) * P],
                                          rows[:, s, k * P:(k + 1) * P], ident_sb[:, :])
                mm.then_inc(t_done, 1)

            def first_product(u, f):
                h = h_bank[f % RING][:, 0:SLOTS]
                for k in range(KC):
                    cols = slice(k * F + f * P, k * F + (f + 1) * P)
                    rows = slice(k * SLOTS, (k + 1) * SLOTS)
                    pe.matmul(h, w_hi[u][:, cols], xt_hi[:, rows], start=(k == 0), stop=False)
                    pe.matmul(h, w_hi[u][:, cols], xt_lo[:, rows], start=False, stop=False)
                    mm = pe.matmul(h, w_lo[u][:, cols], xt_hi[:, rows], start=False, stop=(k == KC - 1))
                if f == FC - 1:
                    mm.then_inc(xt_used, 1)
                if f < RING:
                    mm.then_inc(h_open, 1)

            def second_product(u, f):
                cols = slice(WCOLS + f * D, WCOLS + (f + 1) * D)
                for s in range(SUBS):
                    hi = h_hi[f % RING][:, s * P:(s + 1) * P]
                    lo = h_lo[f % RING][:, s * P:(s + 1) * P]
                    y = y_bank[s][:, 0:D]
                    pe.matmul(y, hi, w_hi[u][:, cols], start=(f == 0), stop=False)
                    pe.matmul(y, hi, w_lo[u][:, cols], start=False, stop=False)
                    mm = pe.matmul(y, lo, w_hi[u][:, cols], start=False, stop=(f == FC - 1))
                    if f == FC - 1:
                        mm.then_inc(y_done, 1)
                if f < FC - RING:
                    mm.then_inc(h_open, 1)

            def one_block(u, u_next, b, weights=None):
                first_product(u, 2)
                first_product(u, 3)
                pe.wait_ge(gathered, b * (16 * SUBS) + 16 * SUBS)
                transpose_block()
                pe.wait_ge(h_ready, b * FC + 1)
                first_product(u, 4)
                pe.wait_ge(h_ready, b * FC + 2)
                second_product(u, 0)
                first_product(u, 5)
                second_product(u, 1)
                pe.wait_ge(h_ready, b * FC + 4)
                first_product(u, 6)
                second_product(u, 2)
                first_product(u, 7)
                second_product(u, 3)
                pe.wait_ge(h_ready, b * FC + 6)
                second_product(u, 4)
                second_product(u, 5)
                if weights is not None:
                    pe.wait_ge(w_lo_done, weights)
                pe.wait_ge(xt_ready, b + 2)
                first_product(u_next, 0)
                pe.wait_ge(h_ready, b * FC + 8)
                second_product(u, 6)
                first_product(u_next, 1)
                second_product(u, 7)

            pe.wait_ge(gathered_first, 16 * SUBS)
            transpose_block(xg_first)
            pe.wait_ge(w_lo_done, PIECES)
            pe.wait_ge(xt_ready, 1)
            for f in range(OPEN):
                first_product(0, f)
            pe.wait_ge(plan_ready, 1)
            with pe.Fori(0, E // 2) as pair:
                for u in range(2):
                    start, end = plan_of(pe, pair * 2 + u)
                    with pe.Fori(start, end - 1) as b:
                        one_block(u, u, b)
                    one_block(u, 1 - u, end - 1, PIECES * (pair * 2 + u + 2))

        @block.scalar
        def _(act):
            act.dma_start(x_sb[0][:, :, :], x_rows[0, :, :, :]).then_inc(x_loaded[0], 16)
            act.dma_start(wr_sb[:, :, :], wr_t.rearrange("(k p) e -> p k e", p=P)).then_inc(const_in, 16)
            for tile, src in ((low_sb, expert_low), (tri_f, tri), (base_sb, slot_base), (ids_sb, token_ids)):
                act.dma_start(tile[:, :], src).then_inc(const_in, 16)
            act.wait_ge(set_dve, 7)
            act.activation(root_t[:, :], var_t[:, :], ACT.Sqrt).then_inc(set_act, 1)

            def split_piece(u, i, n_loaded):
                if i == 0:
                    act.wait_ge(w_loaded, n_loaded)
                cols = slice(i * PIECE, (i + 1) * PIECE)
                act.copy(w_hi[u][:, cols], w_raw[:, cols]).then_inc(w_hi_done, 1)

            for i in range(PIECES):
                split_piece(0, i, 32)

            def stage1(g, u, t):
                act.wait_ge(back_done, g + 1)
                if not (isinstance(t, int) and t == 0):
                    act.wait_ge(hid_stored[u], 16 * t)
                for h in range(2):
                    act.copy(hid_sb[u][:, 2 * h:2 * h + 2, :].rearrange("p j d -> p (j d)"),
                             bank[4 + h][:, :]).then_inc(hid_copied, 1)
                act.wait_ge(hid_copied, 2 * (g + 1))
                act.dma_start(hidden_rows[g, :, :, :], hid_sb[u][:, :, :]).then_inc(hid_stored[u], 16)
                act.wait_ge(gap_ready, g + 1)
                act.activation(ratio[:, :], gap[:, :], ACT.Exp).then_inc(ratio_ready, 1)

            for g in range(2):
                stage1(g, g, 0)
            with act.Fori(1, GROUPS // 2) as t:
                for u in range(2):
                    stage1(t * 2 + u, u, t)

            def split_rows():
                act.copy(xt_hi[:, :], bank[0][:, :]).then_inc(xt_hi_done, 1)

            act.wait_ge(late_in, 16 * 3)
            act.activation(warm_sb[:, :], zero_sb[:, 0:1], ACT.Gelu_apprx_tanh)
            act.wait_ge(t_done, GROUPS + 1)
            split_rows()
            act.wait_ge(plan_ready, 1)

            def gelu(u, b, f):
                act.wait_ge(h_open, b * FC + (f + 1))
                for h in (h_raw, h_hi):
                    ins = act.activation(h[f % RING][:, :], h_bank[f % RING][:, 0:SLOTS], ACT.Gelu_apprx_tanh,
                                         bias=b1_now[u][:, f:f + 1])
                ins.then_inc(gelu_done, 1)

            def one_block(u, e, b, piece0):
                for f in range(FC):
                    gelu(u, b, f)
                    if f == 6:
                        act.wait_ge(xt_used, b + 1)
                        split_rows()
                    if piece0 is not None and f in SPLIT_AT:
                        split_piece(1 - u, piece0 + SPLIT_AT.index(f), 32 * (e + 2))

            with act.Fori(0, E // 2) as pair:
                for u in range(2):
                    e = pair * 2 + u
                    act.copy(b1_now[u][:, :], b1_sb[:, bass.ds(e * FC, FC)]).then_inc(bias_now, 1)
                    act.wait_ge(bias_now, e + 1)
                    start, end = plan_of(act, e)
                    for j in range(2):
                        one_block(u, e, start + j, j * len(SPLIT_AT))
                    with act.Fori(start + 2, end) as b:
                        one_block(u, e, b, None)
            n_all = all_blocks(act)
            for f in range(2):
                gelu(0, n_all, f)

        @block.vector
        def _(dve):
            def by_batch(tile, k, g):
                return tile[:, k, bass.ds(g * GB, GB)].unsqueeze(2).to_broadcast([P, GB, S])

            def scale_x(g):
                dve.wait_ge(t_done, g + 1)
                for k in range(KC):
                    dve.tensor_tensor(xs_t[:, k, :].rearrange("p (b s) -> p b s", s=S),
                                      bank[k][:, :].rearrange("p (b s) -> p b s", s=S),
                                      by_batch(ys_t, k, g), ALU.mult).then_inc(xs_ready, 1)

            dve.memset(zero_sb[:, :], 0.0).then_inc(set_dve, 1)
            dve.memset(ones_sb[:, :], 1.0)
            dve.memset(before[:, :], 0.0)
            dve.wait_ge(first_in, 16 * 3)
            scale = 1.0 / float(np.sqrt(np.float32(D)))
            dve.tensor_tensor(wsq_sb[:, :, :], w_sb[:, :, :], w_sb[:, :, :], ALU.mult).then_inc(set_dve, 1)
            dve.wait_ge(set_pe, 1)
            ys_flat = ys_t[:, :, :].rearrange("p k b -> p (k b)")
            ysq_flat = ysq_t[:, :, :].rearrange("p k b -> p (k b)")
            d_flat = d_t[:, :, :].rearrange("p k b -> p (k b)")
            dve.tensor_scalar(ys_flat, bank[7][:, 0:KC * B], scale, None, ALU.mult).then_inc(set_dve, 1)
            dve.wait_ge(set_dve, 3)
            dve.tensor_tensor(ysq_flat, ys_flat, ys_flat, ALU.mult).then_inc(set_dve, 3)
            scale_x(0)
            dve.wait_ge(set_pe, 2)
            dve.tensor_scalar(var_t[:, :], bank[6][:, 0:KC * B], EPS, None, ALU.add).then_inc(set_dve, 1)
            dve.wait_ge(set_act, 1)
            dve.reciprocal(root_t[:, :], root_t[:, :]).then_inc(set_dve, 1)
            dve.wait_ge(set_dve, 8)
            dve.tensor_tensor(tmp_t[:, :], root_t[:, :], root_t[:, :], ALU.mult).then_inc(set_dve, 1)
            dve.wait_ge(set_dve, 9)
            dve.tensor_tensor(tmp_t[:, :], tmp_t[:, :], var_t[:, :], ALU.mult).then_inc(set_dve, 1)
            dve.wait_ge(set_dve, 10)
            dve.tensor_scalar(tmp_t[:, :], tmp_t[:, :], -0.5, 1.5, ALU.mult, ALU.add).then_inc(set_dve, 1)
            dve.wait_ge(set_dve, 11)
            dve.tensor_tensor(d_flat, tmp_t[:, :], root_t[:, :], ALU.mult).then_inc(set_dve, 1)
            dve.wait_ge(set_dve, 12)

            def split_piece(u, i, count):
                cols = slice(i * PIECE, (i + 1) * PIECE)
                dve.wait_ge(w_hi_done, count)
                dve.tensor_tensor(w_lo[u][:, cols], w_raw[:, cols], w_hi[u][:, cols].bitcast(F32),
                                  ALU.subtract).then_inc(w_lo_done, 1)

            dve.wait_ge(const_in, 16 * CONSTS)
            dve.tensor_copy(tri_sb[:, :], tri_f[:, :]).then_inc(set_dve, 1)

            STEPS = 20

            low3 = low_sb[:, :].unsqueeze(1).to_broadcast(RE)
            base3 = base_sb[:, :].unsqueeze(1).to_broadcast(RE)

            def over_e(a):
                return a.unsqueeze(2).to_broadcast(RE)

            SPLIT_GROUPS = (0, GROUPS - 1)

            def scale_hidden(g):
                for o in range(KC):
                    dve.wait_ge(m_done, KC * g + (o + 1))
                    dve.tensor_tensor(hid_t[:, o, :].rearrange("p (b s) -> p b s", s=S),
                                      bank[2 + o][:, :].rearrange("p (b s) -> p b s", s=S),
                                      by_batch(d_t, o, g), ALU.mult).then_inc(hid_ready, 1)

            def route(g, u, t, choose=True, list_last=True):
                count = [0]

                def mark(ins):
                    count[0] += 1
                    ins.then_inc(step, 1)
                    return count[0]

                def after(n):
                    dve.wait_ge(step, g * STEPS + n)

                def whole(make, *args):
                    with nc.allow_low_precision(reason="whole numbers below 2**24"):
                        return make(*args)

                def begin_list():
                    dve.wait_ge(pos_done, g)
                    if isinstance(g, int) and g - 1 == FILLING:
                        dve.tensor_scalar(filled[:, :], bank[7][:, TILES * E:TILES * E + 1], float(LAG * SLOTS), None,
                                          ALU.is_ge).then_inc(filled_ready, 1)
                    pos = bank[7][:, 0:TILES * E].rearrange("p (j e) -> p j e", e=E)
                    dve.tensor_scalar(over[:, :, :], pos, float(CAP), NO_SLOT, ALU.is_gt, ALU.mult)
                    n = mark(dve.tensor_tensor(slot_e[:, :, :], pos, base3, ALU.add))
                    if choose:
                        k = mark(whole(dve.tensor_reduce, of_group[:, :],
                                       mask[:, :, :].rearrange("p j e -> p e j"), AX_X, ALU.add))
                    dve.wait_ge(ratio_ready, g)
                    m = mark(dve.tensor_scalar(total[:, :], ratio[:, :], 1.0, None, ALU.add))
                    after(n)
                    n = mark(dve.tensor_tensor(slot_e[:, :, :], slot_e[:, :, :], over[:, :, :], ALU.add))
                    after(m)
                    m = mark(dve.reciprocal(total[:, :], total[:, :]))
                    if choose:
                        after(k)
                        dve.tensor_tensor(before[:, :], before[:, :], of_group[:, :], ALU.add).then_inc(counted, 1)
                    if not (isinstance(t, int) and t == 0):
                        dve.wait_ge(scattered[u], (16 * TOP_K * TILES) * t)
                    for c in range(TOP_K):
                        dve.tensor_copy(pay[u][:, c, :, 0], ids_sb[:, bass.ds((g - 1) * TILES, TILES)])
                    after(n)
                    dve.tensor_tensor(picked[:, 0, :, :], first[:, :, :], slot_e[:, :, :], ALU.mult)
                    n = mark(dve.tensor_tensor(picked[:, 1, :, :], second[:, :, :], slot_e[:, :, :], ALU.mult))
                    return n, m

                if list_last:
                    n, m = begin_list()
                if isinstance(g, int) and g in SPLIT_GROUPS:
                    i = SPLIT_GROUPS.index(g)
                    split_piece(0, i, i + 1)
                if choose:
                    dve.wait_ge(l_done, g + 1)
                    one = mark(dve.tensor_copy(logits[:, :, :].rearrange("p j e -> p (j e)"), bank[6][:, 0:TILES * E]))
                if list_last:
                    after(m)
                    gates = pay[u].bitcast(F32)
                    dve.tensor_copy(gates[:, 0, :, 1], total[:, :])
                    dve.tensor_tensor(gates[:, 1, :, 1], total[:, :], ratio[:, :], ALU.mult)
                if choose:
                    after(one)
                    one = mark(dve.tensor_reduce(top[:, 0, :], logits[:, :, :], AX_X, ALU.max))
                if list_last:
                    after(n)
                    n = mark(whole(dve.tensor_reduce, slot_of[:, :, :], picked[:, :, :, :], AX_X, ALU.add))
                if choose:
                    after(one)
                    one = mark(dve.tensor_tensor(hit[:, :, :], logits[:, :, :], over_e(top[:, 0, :]), ALU.is_equal))
                if list_last:
                    after(n)
                    dve.tensor_scalar(low_bits[:, :, :], slot_of[:, :, :], P - 1, None, ALU.bitwise_and)
                    n = mark(dve.tensor_scalar(high_bits[:, :, :], slot_of[:, :, :], P.bit_length() - 1, None,
                                               ALU.arith_shift_right))
                if choose:
                    after(one)
                    one = mark(dve.tensor_tensor(hit[:, :, :], hit[:, :, :], low3, ALU.mult))
                if list_last:
                    after(n)
                    whole(dve.scalar_tensor_tensor, slots[u][:, :, :], low_bits[:, :, :], float(COLS),
                          high_bits[:, :, :], ALU.mult, ALU.add).then_inc(pay_ready, 1)
                if not choose:
                    return
                after(one)
                one = mark(dve.tensor_reduce(low[:, 0, :], hit[:, :, :], AX_X, ALU.min))
                after(one)
                one = mark(dve.tensor_tensor(first[:, :, :], low3, over_e(low[:, 0, :]), ALU.is_equal))
                after(one)
                one = mark(dve.scalar_tensor_tensor(rest[:, :, :], first[:, :, :], -BIG, logits[:, :, :],
                                                    ALU.mult, ALU.add))
                after(one)
                one = mark(dve.tensor_reduce(top[:, 1, :], rest[:, :, :], AX_X, ALU.max))
                after(one)
                one = mark(dve.tensor_tensor(hit[:, :, :], rest[:, :, :], over_e(top[:, 1, :]), ALU.is_equal))
                dve.tensor_tensor(gap[:, :], top[:, 1, :], top[:, 0, :], ALU.subtract).then_inc(gap_ready, 1)
                after(one)
                one = mark(dve.tensor_tensor(hit[:, :, :], hit[:, :, :], low3, ALU.mult))
                after(one)
                one = mark(dve.tensor_reduce(low[:, 1, :], hit[:, :, :], AX_X, ALU.min))
                after(one)
                one = mark(dve.tensor_tensor(second[:, :, :], low3, over_e(low[:, 1, :]), ALU.is_equal))
                after(one)
                ins = dve.tensor_tensor(mask[:, :, :], first[:, :, :], second[:, :, :], ALU.add)
                if STEPS > count[0]:
                    dve.sem_inc(step, STEPS - count[0])
                ins.then_inc(mask_ready, 1)

            def stage1(g, u, t, more=True):
                scale_hidden(g)
                if more:
                    scale_x(g + 1)
                route(g, 1 - u, t - 1 + u, list_last=not (isinstance(g, int) and g == 0))

            for g in range(PEEL):
                stage1(g, g % 2, g // 2)
            with dve.Fori(PEEL // 2, GROUPS // 2 - 1) as t:
                for u in range(2):
                    stage1(t * 2 + u, u, t)
            for g in range(GROUPS - 2, GROUPS):
                stage1(g, g % 2, g // 2, more=(g < GROUPS - 1))
            route(GROUPS, (GROUPS - 1) % 2, (GROUPS - 1) // 2, choose=False)

            dve.wait_ge(late_in, 16 * 3)
            dve.wait_ge(totals_done, 1)
            dve.tensor_tensor(steps_e[:, :, :], bank[6][:, 0:E].unsqueeze(2).to_broadcast([P, E, BLOCKS]),
                              plan_sb[:, 0:BLOCKS].unsqueeze(1).to_broadcast([P, E, BLOCKS]),
                              ALU.is_gt).then_inc(plan_step, 1)
            dve.wait_ge(plan_step, 1)
            dve.tensor_reduce(count_e[:, 0:E], steps_e[:, :, :], AX_X, ALU.add)
            dve.memset(count_e[:, E:E + 1], 0.0).then_inc(plan_step, 1)
            dve.wait_ge(plan_step, 2)
            dve.tensor_scalar(count_e[:, 0:E], count_e[:, 0:E], float(LEAST), None, ALU.max).then_inc(plan_step, 1)
            dve.wait_ge(plan_step, 3)
            dve.tensor_tensor(sums_e[:, :, :], count_e[:, 0:E].unsqueeze(1).to_broadcast([P, E + 1, E]),
                              plan_sb[:, BLOCKS:].rearrange("p (a e) -> p a e", e=E),
                              ALU.mult).then_inc(plan_step, 1)
            dve.wait_ge(plan_step, 4)
            dve.tensor_reduce(before_e[:, :], sums_e[:, :, :], AX_X, ALU.add).then_inc(plan_step, 1)
            dve.tensor_scalar(count_e[:, 0:E], count_e[:, 0:E], -float(LEAST), None, ALU.add).then_inc(plan_step, 1)
            dve.wait_ge(plan_step, 6)
            with nc.allow_low_precision(reason="whole numbers below 2**24"):
                dve.scalar_tensor_tensor(plan[:, 0:E + 1], before_e[:, :], 16.0, count_e[:, :], ALU.mult, ALU.add)
                dve.scalar_tensor_tensor(plan_f[:, :], before_e[:, :], 16.0, count_e[:, :],
                                         ALU.mult, ALU.add).then_inc(plan_step, 1)
                dve.wait_ge(plan_step, 7)
                dve.tensor_scalar(plan[:, E + 1:], plan_f[:, :], -16.0 * LAG, None, ALU.add).then_inc(plan_ready, 1)

            def split_rows(b):
                dve.wait_ge(xt_hi_done, b + 1)
                dve.tensor_tensor(xt_lo[:, :], bank[0][:, :], xt_hi[:, :].bitcast(F32), ALU.subtract).then_inc(xt_ready, 1)

            def split_chunk(b, f):
                dve.wait_ge(gelu_done, b * FC + (f + 1))
                dve.tensor_tensor(h_lo[f % RING][:, :], h_raw[f % RING][:, :],
                                  h_hi[f % RING][:, :].bitcast(F32), ALU.subtract).then_inc(h_ready, 1)

            for i in range(len(SPLIT_GROUPS), PIECES):
                split_piece(0, i, i + 1)
            split_rows(0)
            dve.wait_ge(plan_ready, 1)
            for f in range(2):
                split_chunk(0, f)

            def one_block(u, e, b, tile, piece0):
                for f in range(2, FC):
                    split_chunk(b, f)
                    if f == 6:
                        split_rows(b + 1)
                    if piece0 is not None and f in SPLIT_AT:
                        i = piece0 + SPLIT_AT.index(f)
                        split_piece(1 - u, i, PIECES * (e + 1) + (i + 1))
                split_chunk(b + 1, 0)
                for s in range(SUBS):
                    dve.wait_ge(y_free, b * SUBS + (s + 1))
                    dve.wait_ge(y_done, b * SUBS + (s + 1))
                    dve.tensor_tensor(y_sb[s][:, :], y_bank[s][:, 0:D], b2_sb[:, bass.ds(e * D, D)],
                                      ALU.add).then_inc(y_biased, 1)
                split_chunk(b + 1, 1)
                dve.wait_ge(table_loaded, 16)
                for s in range(SUBS):
                    dve.wait_ge(y_biased, b * SUBS + (s + 1))
                    dve.tensor_scalar(y_sb[s][:, :], y_sb[s][:, :],
                                      table_sb.bitcast(F32)[:, bass.ds(tile + s, 1), 1],
                                      None, ALU.mult).then_inc(y_ready, 1)

            with dve.Fori(0, E // 2) as pair:
                for u in range(2):
                    e = pair * 2 + u
                    start, end = plan_of(dve, e)
                    for j in range(2):
                        one_block(u, e, start + j, e * TILES_E + j * SUBS, j * len(SPLIT_AT))
                    with dve.Fori(start + 2, end) as b:
                        one_block(u, e, b, e * TILES_E + (b - start) * SUBS, None)


def constants():
    p = np.arange(P)
    empty = np.zeros((TABLE, 2), np.int32)
    empty[:, 0] = T + np.arange(TABLE) // COLS + P * (np.arange(TABLE) % COLS % SUBS)
    more_than = np.arange(BLOCKS) * SLOTS
    earlier = np.arange(E)[None, :] < np.arange(E + 1)[:, None]
    return {
        "ident": np.eye(P, dtype=np.float32),
        "tri": (p[:, None] <= p[None, :]).astype(np.float32),
        "expert_low": np.tile(np.arange(E, dtype=np.float32) - E, (P, 1)),
        "slot_base": np.tile(np.arange(E, dtype=np.float32) * CAP - 1, (P, 1)),
        "token_ids": (np.arange(T // P, dtype=np.int32)[None, :] * P + p[:, None].astype(np.int32)),
        "plan_consts": np.tile(np.concatenate([more_than, earlier.ravel()]).astype(np.float32), (P, 1)),
        "empty_table": empty,
    }


def kernel(x, cond_1024, L0_cond_weight, L0_ffn_wr, L0_ffn_w1, L0_ffn_b1, L0_ffn_w2, L0_ffn_b2):
    import concourse.bacc as bacc
    from concourse.bass_utils import run_bass_kernel_spmd

    arrays = {
        "x": x,
        "cond": cond_1024,
        "w": L0_cond_weight,
        "wr_t": np.asarray(L0_ffn_wr).T,
        "w1": L0_ffn_w1,
        "b1_t": np.asarray(L0_ffn_b1).reshape(E, FC, P).transpose(2, 0, 1).reshape(P, E * FC),
        "w2": L0_ffn_w2,
        "b2": L0_ffn_b2,
        **constants(),
    }
    arrays = {f"in_{k}": np.ascontiguousarray(v) for k, v in arrays.items()}
    nc = bacc.Bacc("TRN2", target_bir_lowering=False, num_devices=1)
    args = [nc.dram_tensor(k, v.shape, mybir.dt.from_np(v.dtype), kind="ExternalInput").ap()
            for k, v in arrays.items()]
    out = nc.dram_tensor("out_rows", (T + PAD, D), F32, kind="ExternalOutput").ap()
    build(nc, *args, out)
    r = run_bass_kernel_spmd(nc, [arrays], core_ids=[0])
    return r.results[0]["out_rows"][:T].reshape(B, S, D)
```
